# Optimizing a Trainium2 kernel written in Bass

```python
import numpy as np
import jax
import jax.numpy as jnp

def _softmax(x, axis=-1):
    return jax.nn.softmax(x, axis=axis)

def _gelu(x):
    return jax.nn.gelu(x, approximate=True)

def _silu(x):
    return jax.nn.silu(x)

def _sigmoid(x):
    return jax.nn.sigmoid(x)

def _layernorm(x, axis=-1, eps=1e-05):
    m = jnp.mean(x, axis=axis, keepdims=True)
    v = jnp.var(x, axis=axis, keepdims=True)
    return (x - m) / jnp.sqrt(v + eps)

def _scatter_add(tgt, idx, src, axis=0):
    return tgt.at[idx].add(src)

def _segment_sum(src, seg, n):
    return jax.ops.segment_sum(src, seg, n)
kernel_name = 'mk_xattn_seq_d2_seqx_r2_30660e'

def setup_inputs(seed: int=0):
    np.random.seed(seed)
    _w = jnp.asarray

    def _rec_inputs():
        import jax
        import jax.numpy as jnp
        _rk = jax.random.key(seed)
        x = -0.0002928 + 1 * jax.random.normal(jax.random.fold_in(_rk, 1), (4, 1024, 512), jnp.float32)
        _lenS = 1024 - jax.random.randint(jax.random.fold_in(_rk, 7), (4,), 0, max(1, 1024 // 4) + 1, jnp.int32)
        _lenS2 = 1024 - jax.random.randint(jax.random.fold_in(_rk, 8), (4,), 0, max(1, 1024 // 4) + 1, jnp.int32)
        _ctx_1024P = jax.random.normal(jax.random.fold_in(_rk, 11), (4, 16, 512), jnp.float32)
        _ctx_1024c = jax.random.dirichlet(jax.random.fold_in(_rk, 511), 0.3 * jnp.ones((16,), jnp.float32), (4, 1024))
        _ctx_1024t = jnp.einsum('bsk,bkd->bsd', _ctx_1024c, _ctx_1024P)
        _ctx_1024t = _ctx_1024t * jax.lax.rsqrt(jnp.mean(jnp.square(_ctx_1024t)) + 1e-12) * 0.953939
        ctx_1024 = -1.39393e-06 + 0.999914 * (_ctx_1024t + 0.3 * jax.random.normal(jax.random.fold_in(_rk, 611), (4, 1024, 512), jnp.float32))
        itok_BxS2_0_2047 = jax.random.randint(jax.random.fold_in(_rk, 12), (4, 1024), 0, 1024, jnp.int32)
        _validS = jnp.arange(1024)[None, :] < _lenS[:, None]
        _validS2 = jnp.arange(1024)[None, :] < _lenS2[:, None]
        _causal = jnp.tril(jnp.ones((1024, 1024), dtype=bool))
        mask_BxSxS2_bf0 = jnp.logical_not(jnp.ones((4, 1024, 1024), dtype=bool))
        return (x, ctx_1024, itok_BxS2_0_2047, mask_BxSxS2_bf0)
    x, ctx_1024, itok_BxS2_0_2047, mask_BxSxS2_bf0 = _rec_inputs()

    def _L0_xattn_setup():
        import jax, jax.numpy as jnp
        import numpy as np
        B, S, D_MODEL, H, D_FF = (2, 1024, 512, 16, 2048)
        D_HEAD = D_MODEL // H
        LN_EPS = 1e-05

        def _xavier(key, shape):
            fan_out, fan_in = shape
            std = (2.0 / (fan_in + fan_out)) ** 0.5
            return jax.random.normal(key, shape, dtype=jnp.float32) * std

        def _layer_norm(x, g, b):
            mu = jnp.mean(x, axis=-1, keepdims=True)
            var = jnp.mean((x - mu) ** 2, axis=-1, keepdims=True)
            return (x - mu) * jax.lax.rsqrt(var + LN_EPS) * g + b
        key = jax.random.key(seed)
        ks = jax.random.split(key, 8)
        return {'q': jax.random.normal(ks[0], (B, S, D_MODEL), dtype=jnp.float32), 'k': jax.random.normal(ks[1], (B, S, D_MODEL), dtype=jnp.float32), 'Wq': _xavier(ks[2], (D_MODEL, D_MODEL)), 'bq': jnp.zeros((D_MODEL,), jnp.float32), 'Wk': _xavier(ks[3], (D_MODEL, D_MODEL)), 'bk': jnp.zeros((D_MODEL,), jnp.float32), 'Wv': _xavier(ks[4], (D_MODEL, D_MODEL)), 'bv': jnp.zeros((D_MODEL,), jnp.float32), 'W1': _xavier(ks[5], (D_FF, D_MODEL)), 'b1': jnp.zeros((D_FF,), jnp.float32), 'W2': _xavier(ks[6], (D_MODEL, D_FF)), 'b2': jnp.zeros((D_MODEL,), jnp.float32), 'ln_g': jnp.ones((D_MODEL,), jnp.float32), 'ln_b': jnp.zeros((D_MODEL,), jnp.float32), 'use_causal_mask': 1}
    _L0_xattn_all = _L0_xattn_setup()
    _L0_xattn_in = {k: v for k, v in _L0_xattn_all.items() if k in ('Wq', 'bq', 'Wk', 'bk', 'Wv', 'bv', 'W1', 'b1', 'W2', 'b2', 'ln_g', 'ln_b')}
    del _L0_xattn_all

    def _L1_xattn_setup():
        import jax, jax.numpy as jnp
        import numpy as np
        EMBED = 512
        HEADS = 16
        HEAD_DIM = EMBED // HEADS
        MAX_POS = 1024
        BASE = 10000.0
        SCALE = HEAD_DIM ** (-0.5)

        def _rope_tables():
            inv_freq = 1.0 / BASE ** (jnp.arange(0, HEAD_DIM, 2, dtype=jnp.float32) / HEAD_DIM)
            freqs = jnp.arange(MAX_POS, dtype=jnp.float32)[:, None] * inv_freq[None]
            emb = jnp.concatenate([freqs, freqs], axis=-1)
            return (jnp.cos(emb), jnp.sin(emb))

        def _rotate_half(x):
            x1, x2 = (x[..., :x.shape[-1] // 2], x[..., x.shape[-1] // 2:])
            return jnp.concatenate([-x2, x1], axis=-1)

        def _apply_rope(x, pos, cos_t, sin_t):
            cos = cos_t[pos][:, None]
            sin = sin_t[pos][:, None]
            return x * cos + _rotate_half(x) * sin
        key = jax.random.key(seed)
        ks = jax.random.split(key, 10)
        B, N, M, C = (2, 1024, 1024, EMBED)
        w_std = (2.0 / (C + C)) ** 0.5
        return {'query': jax.random.normal(ks[0], (B, N, C), jnp.float32), 'key': jax.random.normal(ks[1], (B, M, C), jnp.float32), 'value': jax.random.normal(ks[2], (B, M, C), jnp.float32), 'query_pos': jax.random.randint(ks[3], (B, N), 0, MAX_POS, jnp.int32), 'key_pos': jax.random.randint(ks[4], (B, M), 0, MAX_POS, jnp.int32), 'attn_mask': jnp.zeros((B, N, M), jnp.bool_), 'q_w': jax.random.normal(ks[5], (C, C), jnp.float32) * w_std, 'q_b': jnp.zeros((C,), jnp.float32), 'k_w': jax.random.normal(ks[6], (C, C), jnp.float32) * w_std, 'v_w': jax.random.normal(ks[7], (C, C), jnp.float32) * w_std, 'v_b': jnp.zeros((C,), jnp.float32), 'proj_w': jax.random.normal(ks[8], (C, C), jnp.float32) * w_std, 'proj_b': jnp.zeros((C,), jnp.float32)}
    _L1_xattn_all = _L1_xattn_setup()
    _L1_xattn_in = {k: v for k, v in _L1_xattn_all.items() if k in ('q_w', 'q_b', 'k_w', 'v_w', 'v_b', 'proj_w', 'proj_b')}
    del _L1_xattn_all
    return {'x': x, 'ctx_1024': ctx_1024, 'itok_BxS2_0_2047': itok_BxS2_0_2047, 'mask_BxSxS2_bf0': mask_BxSxS2_bf0, 'L0_xattn_Wq': _L0_xattn_in['Wq'], 'L0_xattn_bq': _L0_xattn_in['bq'], 'L0_xattn_Wk': _L0_xattn_in['Wk'], 'L0_xattn_bk': _L0_xattn_in['bk'], 'L0_xattn_Wv': _L0_xattn_in['Wv'], 'L0_xattn_bv': _L0_xattn_in['bv'], 'L0_xattn_W1': _L0_xattn_in['W1'], 'L0_xattn_b1': _L0_xattn_in['b1'], 'L0_xattn_W2': _L0_xattn_in['W2'], 'L0_xattn_b2': _L0_xattn_in['b2'], 'L0_xattn_ln_g': _L0_xattn_in['ln_g'], 'L0_xattn_ln_b': _L0_xattn_in['ln_b'], 'L1_xattn_q_w': _L1_xattn_in['q_w'], 'L1_xattn_q_b': _L1_xattn_in['q_b'], 'L1_xattn_k_w': _L1_xattn_in['k_w'], 'L1_xattn_v_w': _L1_xattn_in['v_w'], 'L1_xattn_v_b': _L1_xattn_in['v_b'], 'L1_xattn_proj_w': _L1_xattn_in['proj_w'], 'L1_xattn_proj_b': _L1_xattn_in['proj_b']}

def reference(x, ctx_1024, itok_BxS2_0_2047, mask_BxSxS2_bf0, L0_xattn_Wq, L0_xattn_bq, L0_xattn_Wk, L0_xattn_bk, L0_xattn_Wv, L0_xattn_bv, L0_xattn_W1, L0_xattn_b1, L0_xattn_W2, L0_xattn_b2, L0_xattn_ln_g, L0_xattn_ln_b, L1_xattn_q_w, L1_xattn_q_b, L1_xattn_k_w, L1_xattn_v_w, L1_xattn_v_b, L1_xattn_proj_w, L1_xattn_proj_b):
    import jax
    import jax.numpy as jnp

    def _L0_xattn_ref(q, k, Wq, bq, Wk, bk, Wv, bv, W1, b1, W2, b2, ln_g, ln_b, use_causal_mask):
        import jax, jax.numpy as jnp
        import numpy as np
        B, S, D_MODEL, H, D_FF = (2, 1024, 512, 16, 2048)
        D_HEAD = D_MODEL // H
        LN_EPS = 1e-05

        def _xavier(key, shape):
            fan_out, fan_in = shape
            std = (2.0 / (fan_in + fan_out)) ** 0.5
            return jax.random.normal(key, shape, dtype=jnp.float32) * std

        def _layer_norm(x, g, b):
            mu = jnp.mean(x, axis=-1, keepdims=True)
            var = jnp.mean((x - mu) ** 2, axis=-1, keepdims=True)
            return (x - mu) * jax.lax.rsqrt(var + LN_EPS) * g + b
        Bq, Sq, _ = q.shape
        Sk = k.shape[1]
        Q = q @ Wq.T + bq
        K = k @ Wk.T + bk
        V = k @ Wv.T + bv
        Q_ = Q.reshape(Bq, Sq, H, D_HEAD).transpose(0, 2, 1, 3)
        K_ = K.reshape(Bq, Sk, H, D_HEAD).transpose(0, 2, 1, 3)
        V_ = V.reshape(Bq, Sk, H, D_HEAD).transpose(0, 2, 1, 3)
        scores = jnp.einsum('bhqd,bhkd->bhqk', Q_, K_) / D_HEAD ** 0.5
        if use_causal_mask:
            causal = jnp.tril(jnp.ones((Sq, Sk), dtype=bool))
            scores = jnp.where(causal, scores, jnp.float32(-1000000000.0))
        sim = jax.nn.softmax(scores, axis=-1)
        att = jnp.einsum('bhqk,bhkd->bhqd', sim, V_)
        att_h = att.transpose(0, 2, 1, 3).reshape(Bq, Sq, D_MODEL)
        att_h = att_h + q
        att_h = _layer_norm(att_h, ln_g, ln_b)
        ff = jax.nn.gelu(att_h @ W1.T + b1, approximate=False) @ W2.T + b2
        return ff + att_h

    def _L1_xattn_ref(query, key, value, query_pos, key_pos, attn_mask, q_w, q_b, k_w, v_w, v_b, proj_w, proj_b):
        import jax, jax.numpy as jnp
        import numpy as np
        EMBED = 512
        HEADS = 16
        HEAD_DIM = EMBED // HEADS
        MAX_POS = 1024
        BASE = 10000.0
        SCALE = HEAD_DIM ** (-0.5)

        def _rope_tables():
            inv_freq = 1.0 / BASE ** (jnp.arange(0, HEAD_DIM, 2, dtype=jnp.float32) / HEAD_DIM)
            freqs = jnp.arange(MAX_POS, dtype=jnp.float32)[:, None] * inv_freq[None]
            emb = jnp.concatenate([freqs, freqs], axis=-1)
            return (jnp.cos(emb), jnp.sin(emb))

        def _rotate_half(x):
            x1, x2 = (x[..., :x.shape[-1] // 2], x[..., x.shape[-1] // 2:])
            return jnp.concatenate([-x2, x1], axis=-1)

        def _apply_rope(x, pos, cos_t, sin_t):
            cos = cos_t[pos][:, None]
            sin = sin_t[pos][:, None]
            return x * cos + _rotate_half(x) * sin
        B, N, C = query.shape
        M = key.shape[1]
        cos_t, sin_t = _rope_tables()
        q = (query @ q_w + q_b).reshape(B, N, HEADS, HEAD_DIM).transpose(0, 2, 1, 3)
        k = (key @ k_w).reshape(B, M, HEADS, HEAD_DIM).transpose(0, 2, 1, 3)
        v = (value @ v_w + v_b).reshape(B, M, HEADS, HEAD_DIM).transpose(0, 2, 1, 3)
        q = _apply_rope(q, query_pos, cos_t, sin_t)
        k = _apply_rope(k, key_pos, cos_t, sin_t)
        attn = jnp.einsum('bhnc,bhmc->bhnm', q, k) * SCALE
        attn = jnp.where(attn_mask[:, None], -jnp.inf, attn)
        attn = jax.nn.softmax(attn, axis=-1)
        x = jnp.einsum('bhnm,bhmd->bhnd', attn, v).transpose(0, 2, 1, 3).reshape(B, N, C)
        x = x @ proj_w + proj_b
        return x + query
    x = _L0_xattn_ref(x, ctx_1024, L0_xattn_Wq, L0_xattn_bq, L0_xattn_Wk, L0_xattn_bk, L0_xattn_Wv, L0_xattn_bv, L0_xattn_W1, L0_xattn_b1, L0_xattn_W2, L0_xattn_b2, L0_xattn_ln_g, L0_xattn_ln_b, 1)
    x = _L1_xattn_ref(x, ctx_1024, ctx_1024, itok_BxS2_0_2047, itok_BxS2_0_2047, mask_BxSxS2_bf0, L1_xattn_q_w, L1_xattn_q_b, L1_xattn_k_w, L1_xattn_v_w, L1_xattn_v_b, L1_xattn_proj_w, L1_xattn_proj_b)
    return x

_drawn_inputs = setup_inputs


def setup_inputs(seed=0):
    import zlib

    import numpy as np

    out = dict(_drawn_inputs(seed))
    spreads = {'L0_xattn_bq': (0.0, 0.49),
     'L0_xattn_bk': (0.0, 0.8),
     'L0_xattn_bv': (0.0, 0.1),
     'L0_xattn_b1': (0.0, 0.1),
     'L0_xattn_b2': (0.0, 0.1),
     'L0_xattn_ln_g': (1.0, 0.2),
     'L0_xattn_ln_b': (0.0, 0.1),
     'L1_xattn_q_b': (0.0, 0.631),
     'L1_xattn_v_b': (0.0, 0.1),
     'L1_xattn_proj_b': (0.0, 0.1)}
    factors = {}
    for name, (base, spread) in spreads.items():
        noise = np.random.default_rng([zlib.crc32(name.encode()), seed]).standard_normal(out[name].shape)
        drawn = base * np.exp(spread * noise) if base else spread * noise
        out[name] = jnp.asarray(drawn.astype(out[name].dtype))
    for name, factor in factors.items():
        out[name] = (out[name] * factor).astype(out[name].dtype)
    return out
```

```python
from contextlib import ExitStack

import numpy as np

import concourse.bass as bass
from concourse import mybir

FP32 = mybir.dt.float32
F32R = mybir.dt.float32r
BF16 = mybir.dt.bfloat16
U8 = mybir.dt.uint8
U32 = mybir.dt.uint32
I32 = mybir.dt.int32
ALU = mybir.AluOpType
ACT = mybir.ActivationFunctionType
AX = mybir.AxisListType

P = 128
B, S, D = 4, 1024, 512
H, DH = 16, 32
FF = 2048
MAX_POS = 1024
KT = D // P
CH = 512
NCH = S // CH
PAIRS = H // 2
NSTEP = B * PAIRS
KB = S // P
BIG = 1.0e30
FLOOR = -0.5 * BIG
SCALE = float(DH) ** -0.5
LN_EPS = 1e-5
NB = 8
STAGES = 4


class Places:

    def __init__(self, nc, ctx, tag):
        self.nc, self.ctx, self.tag = nc, ctx, tag
        self.handles = []

    def clear(self):
        self.nc.clear_and_free_semaphores(self.handles)
        self.nc.all_engine_barrier()

    def block(self):
        self.ctx.callback(self.clear)
        return self.ctx.enter_context(self.nc.Block())

    def sb(self, name, shape, dtype=FP32):
        return self.ctx.enter_context(self.nc.sbuf_tensor(f"{self.tag}_{name}", shape, dtype))

    def ps(self, name, shape):
        return self.ctx.enter_context(self.nc.psum_tensor(f"{self.tag}_{name}", shape, FP32))

    def sem(self, name):
        self.handles.append(self.nc.alloc_semaphore(f"{self.tag}_{name}"))
        return self.handles[-1]

    def sems(self, name, n):
        return [self.sem(f"{name}{i}") for i in range(n)]


def prepare_tables(nc, tag, itok, trig, mask, cs_dram, mask_dram, any_dram):
    NT = B * KB
    GATHERS = 8
    with ExitStack() as ctx:
        m = Places(nc, ctx, tag)
        index = m.sb("index", [P, NT], U32)
        rows = m.sb("rows", [P, GATHERS, 2 * P])
        turned = m.sb("turned", [P, 2, 2, P])
        ident = m.sb("ident", [P, P])
        bits = m.sb("bits", [P, 2, 2, S], U8)
        addend = m.sb("addend", [P, 2, 2, S], BF16)
        most = m.sb("most", [P, B * KB // 2 + 1])
        ones = m.sb("ones", [P, 1])
        any_masked = m.sb("any_masked", [1, 1], I32)
        bank = m.ps("bank", [P, 2, 512])
        total = m.ps("total", [P, 512])
        index_loaded = m.sem("index_loaded")
        ident_ready = m.sem("ident_ready")
        rows_loaded = m.sems("rows_loaded", GATHERS)
        rows_turned = m.sem("rows_turned")
        turned_ready = m.sem("turned_ready")
        turned_stored = m.sems("turned_stored", 2)
        bits_loaded = m.sems("bits_loaded", 2)
        addend_ready = m.sem("addend_ready")
        addend_stored = m.sems("addend_stored", 2)
        most_ready = m.sem("most_ready")
        total_ready = m.sem("total_ready")
        any_ready = m.sem("any_ready")
        any_stored = m.sem("any_stored")
        block = m.block()
        MT = B * KB // 2

        @block.gpsimd
        def _(pool):
            pool.dma_start(index[:, :], itok[:, :]).then_inc(index_loaded, 16)
            pool.memset(ident[:, :], 0.0).then_inc(ident_ready, 1)
            pool.wait_ge(ident_ready, 1)
            pool.affine_select(out=ident[:, :], in_=ident[:, :], compare_op=ALU.not_equal, fill=1.0, base=0,
                               pattern=[[-1, P]], channel_multiplier=1).then_inc(ident_ready, 1)
            pool.wait_ge(index_loaded, 16)
            for t in range(NT):
                if t >= GATHERS:
                    pool.wait_ge(rows_turned, t - GATHERS + 1)
                pool.indirect_dma_start(out=rows[:, t % GATHERS, :], out_offset=None, in_=trig[:, :],
                                        in_offset=bass.IndirectOffsetOnAxis(ap=index[:, t:t + 1], axis=0)
                                        ).then_inc(rows_loaded[t % GATHERS], 16)

        @block.tensor
        def _(pe):
            pe.wait_ge(ident_ready, 2)
            for t in range(NT):
                pe.wait_ge(rows_loaded[t % GATHERS], 16 * (t // GATHERS + 1))
                if t >= 2:
                    pe.wait_ge(turned_ready, t - 1)
                for c in range(2):
                    last = nc.tensor.transpose(bank[:, t % 2, c * P:(c + 1) * P], rows[:, t % GATHERS, c * P:(c + 1) * P],
                                               ident[:, :])
                last.then_inc(rows_turned, 1)
            pe.wait_ge(most_ready, MT + 2)
            nc.tensor.matmul(total[0:1, 0:1], most[:, MT:MT + 1], ones[:, :], start=True, stop=True).then_inc(total_ready, 1)

        @block.scalar
        def _(act):
            for t in range(NT):
                act.wait_ge(rows_turned, t + 1)
                if t >= 2:
                    act.wait_ge(turned_stored[t % 2], 16 * (t // 2))
                nc.scalar.activation(turned[:, t % 2, :, :], bank[:, t % 2, 0:2 * P].rearrange("p (c n) -> p c n", c=2),
                                     ACT.Copy).then_inc(turned_ready, 1)

        @block.sync
        def _(sp):
            for t in range(NT):
                if t < MT:
                    if t >= 2:
                        sp.wait_ge(addend_ready, t - 1)
                    sp.dma_start(bits[:, t % 2, :, :], mask[2 * t:2 * t + 2, :, :].rearrange("t p k -> p t k")
                                 ).then_inc(bits_loaded[t % 2], 16)
                sp.wait_ge(turned_ready, t + 1)
                sp.dma_start(cs_dram[:, :, t * P:(t + 1) * P].rearrange("c p n -> p c n"), turned[:, t % 2, :, :]
                             ).then_inc(turned_stored[t % 2], 16)
                if t < MT:
                    sp.wait_ge(addend_ready, t + 1)
                    sp.dma_start(mask_dram[2 * t:2 * t + 2, :, :].rearrange("t p k -> p t k"), addend[:, t % 2, :, :]
                                 ).then_inc(addend_stored[t % 2], 16)
            sp.wait_ge(any_ready, 1)
            sp.dma_start(any_dram, any_masked[:, :]).then_inc(any_stored, 16)
            sp.wait_ge(any_stored, 16)
            for n in range(2):
                sp.wait_ge(turned_stored[n], 16 * (NT // 2))
                sp.wait_ge(addend_stored[n], 16 * (MT // 2))

        @block.vector
        def _(dve):
            for t in range(MT):
                dve.wait_ge(bits_loaded[t % 2], 16 * (t // 2 + 1))
                if t >= 2:
                    dve.wait_ge(addend_stored[t % 2], 16 * (t // 2))
                nc.vector.tensor_reduce(most[:, t:t + 1], bits[:, t % 2, :, :], AX.XY, ALU.max).then_inc(most_ready, 1)
                nc.vector.tensor_scalar(addend[:, t % 2, :, :], bits[:, t % 2, :, :], -BIG, None, ALU.mult
                                        ).then_inc(addend_ready, 1)
            dve.memset(ones[:, :], 1.0).then_inc(most_ready, 1)
            dve.wait_ge(most_ready, MT + 1)
            nc.vector.tensor_reduce(most[:, MT:MT + 1], most[:, 0:MT], AX.X, ALU.max).then_inc(most_ready, 1)
            dve.wait_ge(total_ready, 1)
            nc.vector.tensor_copy(any_masked[:, :], total[0:1, 0:1]).then_inc(any_ready, 1)


def by_head(inverses, b, c, to):
    parts = P // DH
    heads = inverses[bass.ds(b * H, H), c].rearrange("(k j) n -> j k n", j=parts)
    return [(to[j * DH:(j + 1) * DH, :, :], heads[j].unsqueeze(0).to_broadcast([DH, KT, c.stop - c.start]))
            for j in range(parts)]


def project(nc, tag, sources, jobs, trig_dram=None):
    NW, NS = len(jobs), len(sources)
    NTILE = KT * NW
    BODY = NCH * NTILE
    ROUNDS = BODY // NB
    assert BODY % NB == 0 and BODY % STAGES == 0
    normed = sources[0][1] is not None
    rotary = [k for k, job in enumerate(jobs) if job[0] == "r"]
    residual = next((job[4][1] for job in jobs if job[0] == "o"), None)
    ROPE_OPS = 6

    def kind(g):
        return jobs[g % NTILE // KT][0]

    def tiles(hf):
        return [(hf * NTILE + k * KT + t, k, t) for k in range(NW) for t in range(KT)]

    def splits_before(g):
        return sum(kind(n) in "tr" for n in range(g))

    def pairs_before(g):
        return sum(kind(n) == "r" for n in range(g)) // 2

    def stores(slot, upto):
        return sum((32 if kind(n) in "tr" else 16) for n in range(slot, upto, STAGES))

    def following(b, hf):
        return (b, hf + 1) if hf + 1 < NCH else ((b + 1) % B, 0)

    with ExitStack() as ctx:
        m = Places(nc, ctx, tag)
        w_raw = m.sb("w_raw", [P, KT, D])
        w_hi = [m.sb(f"w_hi{k}", [P, KT, D], F32R) for k in range(NW)]
        w_lo = [m.sb(f"w_lo{k}", [P, KT, D], F32R) for k in range(NW)]
        raw = [m.sb(f"raw{s}", [P, KT, CH]) for s in range(NS)]
        s_hi = [m.sb(f"s_hi{s}", [P, 2, KT, CH], F32R) for s in range(NS)]
        s_lo = [m.sb(f"s_lo{s}", [P, 2, KT, CH], F32R) for s in range(NS)]
        full = m.sb("full", [P, STAGES, CH])
        hi = m.sb("hi", [P, STAGES, CH], F32R)
        lo = m.sb("lo", [P, STAGES, CH], F32R)
        inverse = m.sb("inverse", [P, KT, CH]) if normed else None
        packed = m.sb("packed", [P, B * H * S // P]) if normed else None
        trig = m.sb("trig", [P, 2, CH]) if rotary else None
        turn = m.sb("turn", [P, 2, CH]) if rotary else None
        res = m.sb("res", [P, 2, KT, CH]) if residual is not None else None
        bias = {k: m.sb(f"bias{k}", [P, D] if job[0] == "v" else [P, KT])
                for k, job in enumerate(jobs) if job[3] is not None}
        bank = m.ps("bank", [P, NB, CH])
        w_loaded = m.sem("w_loaded")
        w_hi_ready = m.sem("w_hi_ready")
        w_ready = m.sem("w_ready")
        bias_loaded = m.sem("bias_loaded")
        raw_loaded = m.sems("raw_loaded", NS)
        packed_loaded = m.sem("packed_loaded")
        packed_ready = m.sem("packed_ready")
        packed_stored = m.sem("packed_stored")
        inverse_loaded = m.sem("inverse_loaded")
        normed_ready = m.sem("normed_ready")
        hi_ready = m.sems("hi_ready", NS)
        lo_ready = m.sems("lo_ready", NS)
        trig_loaded = m.sem("trig_loaded")
        res_loaded = m.sems("res_loaded", NCH)
        tile_ready = m.sem("tile_ready")
        bank_out = m.sems("bank_out", NB)
        rope_done = m.sem("rope_done")
        tile_hi = m.sem("tile_hi")
        tile_split = m.sem("tile_split")
        stored = m.sems("stored", STAGES)
        block = m.block()

        def out_of_bank(b, g):
            return b * ROUNDS + (g // NB + 1)

        @block.sync
        def _(sp):
            for k, job in enumerate(jobs):
                if k:
                    sp.wait_ge(w_ready, k)
                sp.dma_start(w_raw[:, :, :], job[2].rearrange("(k p) n -> p k n", p=P)).then_inc(w_loaded, 16)
                if k in bias:
                    sp.dma_start(bias[k][:, :], job[3]).then_inc(bias_loaded, 16)
            with sp.Fori(0, B) as b:
                for hf in range(NCH):
                    c = slice(hf * CH, (hf + 1) * CH)
                    for g, k, t in tiles(hf):
                        what, outs, slot = jobs[k][0], jobs[k][4], g % STAGES
                        if what in "tr":
                            sp.wait_ge(tile_split, b * splits_before(BODY) + splits_before(g) + 1)
                            for part, dram in ((hi, outs[0]), (lo, outs[1])):
                                if what == "t":
                                    to = dram[bass.ds(b * D + t * P, P), c]
                                else:
                                    to = dram[bass.ds(b * D + (t // 2) * 2 * P, 2 * P), c].rearrange(
                                        "(h two s) n -> two h s n", two=2, s=DH // 2)[t % 2]
                                sp.dma_start(to, part[:, slot, :].bitcast(FP32)).then_inc(stored[slot], 16)
                            continue
                        sp.wait_ge(bank_out[g % NB], out_of_bank(b, g))
                        if what == "v":
                            rows = slice(hf * CH + t * P, hf * CH + (t + 1) * P)
                            to = outs[0][bass.ds(b * PAIRS, PAIRS), rows, :].rearrange("a p d -> p a d")
                            sp.dma_start(to, full[:, slot, :].rearrange("p (a d) -> p a d", a=PAIRS)
                                         ).then_inc(stored[slot], 16)
                        else:
                            sp.dma_start(outs[0][bass.ds(b * D + t * P, P), c], full[:, slot, :]
                                         ).then_inc(stored[slot], 16)
            for slot in range(STAGES):
                sp.wait_ge(stored[slot], B * stores(slot, BODY))

        @block.gpsimd
        def _(pool):
            def load_and_split(b, hf, n):
                c = slice(hf * CH, (hf + 1) * CH)
                for s, (raw_dram, sums_dram) in enumerate(sources):
                    pool.wait_ge(lo_ready[s], n)
                    pool.nop(nofuse=True)
                    pool.dma_start(raw[s][:, :, :], raw_dram[bass.ds(b * D, D), c].rearrange("(k p) n -> p k n", p=P)
                                   ).then_inc(raw_loaded[s], 16)
                    if normed:
                        for to, src in by_head(sums_dram[1], b, c, inverse):
                            pool.dma_start(to, src).then_inc(inverse_loaded, 16)
                for s in range(NS):
                    pool.wait_ge(hi_ready[s], n + 1)
                    nc.gpsimd.tensor_tensor(s_lo[s][:, hf, :, :], raw[s][:, :, :], s_hi[s][:, hf, :, :].bitcast(FP32),
                                            ALU.subtract).then_inc(lo_ready[s], 1)

            if normed:
                lines = "r (c n) -> (r c) n"
                sums_dram, inverse_dram = (x.rearrange(lines, c=P // (B * H)) for x in sources[0][1])
                pool.dma_start(packed[:, :], sums_dram).then_inc(packed_loaded, 16)
                pool.wait_ge(packed_ready, 1)
                pool.dma_start(inverse_dram, packed[:, :]).then_inc(packed_stored, 16)
                pool.wait_ge(packed_stored, 16)
            load_and_split(0, 0, 0)
            with pool.Fori(0, B) as b:
                for hf in range(NCH):
                    n = b * NCH + hf
                    c = slice(hf * CH, (hf + 1) * CH)
                    if rotary:
                        pool.wait_ge(rope_done, n * (2 * len(rotary) * ROPE_OPS))
                        pool.dma_start(trig[:, :, :], trig_dram[:, :, bass.ds(b * S + hf * CH, CH)].rearrange(
                            "c p n -> p c n")).then_inc(trig_loaded, 16)
                    if residual is not None:
                        last = hf * NTILE + NTILE - 1
                        pool.wait_ge(bank_out[last % NB], b * ROUNDS)
                        pool.nop(nofuse=True)
                        pool.dma_start(res[:, hf, :, :], residual[bass.ds(b * D, D), c].rearrange(
                            "(k p) n -> p k n", p=P)).then_inc(res_loaded[hf], 16)
                    load_and_split(*following(b, hf), n + 1)
                    for g, k, t in tiles(hf):
                        if k not in rotary or t % 2:
                            continue
                        q = b * pairs_before(BODY) + pairs_before(g)
                        pool.wait_ge(trig_loaded, (n + 1) * 16)
                        for half in (g, g + 1):
                            pool.wait_ge(bank_out[half % NB], out_of_bank(b, half))
                        pool.wait_ge(tile_split, b * splits_before(BODY) + splits_before(g))
                        first, second = full[:, g % STAGES, :], full[:, (g + 1) % STAGES, :]
                        cos, sin = trig[:, 0, :], trig[:, 1, :]
                        for r, (o, x, y, op) in enumerate((
                            (turn[:, 0, :], first, cos, ALU.mult),
                            (turn[:, 1, :], second, sin, ALU.mult),
                            (turn[:, 0, :], turn[:, 0, :], turn[:, 1, :], ALU.subtract),
                            (turn[:, 1, :], first, sin, ALU.mult),
                            (second, second, cos, ALU.mult),
                            (second, second, turn[:, 1, :], ALU.add),
                        )):
                            if r in (2, 3, 5):
                                pool.wait_ge(rope_done, q * ROPE_OPS + r)
                            nc.gpsimd.tensor_tensor(o, x, y, op).then_inc(rope_done, 1)

        @block.scalar
        def _(act):
            def high_parts(hf, n, tiles_before):
                if tiles_before is not None:
                    act.wait_ge(tile_ready, tiles_before)
                for s in range(NS):
                    if normed:
                        act.wait_ge(normed_ready, n + 1)
                    else:
                        act.wait_ge(raw_loaded[s], (n + 1) * 16)
                    nc.scalar.activation(s_hi[s][:, hf, :, :], raw[s][:, :, :], ACT.Copy).then_inc(hi_ready[s], 1)

            high_parts(0, 0, None)
            if bias:
                act.wait_ge(bias_loaded, 16 * len(bias))
            with act.Fori(0, B) as b:
                for hf in range(NCH):
                    high_parts((hf + 1) % NCH, b * NCH + hf + 1, b * BODY + hf * NTILE)
                    for g, k, t in tiles(hf):
                        if kind(g) not in "tr":
                            continue
                        slot = g % STAGES
                        act.wait_ge(tile_ready, b * BODY + g + 1)
                        act.wait_ge(stored[slot], b * stores(slot, BODY) + stores(slot, g))
                        if k in bias:
                            nc.scalar.activation(full[:, slot, :], bank[:, g % NB, :], ACT.Identity, bias=bias[k][:, t:t + 1]
                                                 ).then_inc(bank_out[g % NB], 1)
                        else:
                            nc.scalar.activation(full[:, slot, :], bank[:, g % NB, :], ACT.Copy
                                                 ).then_inc(bank_out[g % NB], 1)

        @block.vector
        def _(dve):
            def normalise(n):
                dve.wait_ge(inverse_loaded, (n + 1) * (P // DH * 16))
                dve.wait_ge(raw_loaded[0], (n + 1) * 16)
                nc.vector.tensor_tensor(raw[0][:, :, :], raw[0][:, :, :], inverse[:, :, :], ALU.mult).then_inc(normed_ready, 1)

            if normed:
                dve.wait_ge(packed_loaded, 16)
                nc.vector.reciprocal(packed[:, :], packed[:, :]).then_inc(packed_ready, 1)
                normalise(0)
            for k in range(NW):
                dve.wait_ge(w_loaded, 16 * (k + 1))
                nc.vector.tensor_copy(w_hi[k][:, :, :], w_raw[:, :, :]).then_inc(w_hi_ready, 1)
                dve.wait_ge(w_hi_ready, k + 1)
                nc.vector.tensor_tensor(w_lo[k][:, :, :], w_raw[:, :, :], w_hi[k][:, :, :].bitcast(FP32),
                                        ALU.subtract).then_inc(w_ready, 1)
            if bias:
                dve.wait_ge(bias_loaded, 16 * len(bias))
            with dve.Fori(0, B) as b:
                for hf in range(NCH):
                    if normed:
                        normalise(b * NCH + hf + 1)
                    for g, k, t in tiles(hf):
                        what, slot = jobs[k][0], g % STAGES
                        if what in "tr":
                            e = b * splits_before(BODY) + splits_before(g)
                            if what == "t":
                                dve.wait_ge(bank_out[g % NB], out_of_bank(b, g))
                                src = full[:, slot, :]
                            else:
                                q = b * pairs_before(BODY) + pairs_before(g - t % 2)
                                dve.wait_ge(rope_done, q * ROPE_OPS + ROPE_OPS)
                                src = turn[:, 0, :] if t % 2 == 0 else full[:, slot, :]
                            dve.wait_ge(stored[slot], b * stores(slot, BODY) + stores(slot, g))
                            nc.vector.tensor_copy(hi[:, slot, :], src).then_inc(tile_hi, 1)
                            dve.wait_ge(tile_hi, e + 1)
                            nc.vector.tensor_tensor(lo[:, slot, :], src, hi[:, slot, :].bitcast(FP32), ALU.subtract
                                                    ).then_inc(tile_split, 1)
                            continue
                        dve.wait_ge(tile_ready, b * BODY + g + 1)
                        dve.wait_ge(stored[slot], b * stores(slot, BODY) + stores(slot, g))
                        if what == "v":
                            nc.vector.tensor_tensor(full[:, slot, :], bank[:, g % NB, :], bias[k][:, :], ALU.add
                                                    ).then_inc(bank_out[g % NB], 1)
                        else:
                            dve.wait_ge(res_loaded[hf], b * 16 + 16)
                            nc.vector.scalar_tensor_tensor(full[:, slot, :], bank[:, g % NB, :], bias[k][:, t:t + 1],
                                                           res[:, hf, t, :], ALU.add, ALU.add
                                                           ).then_inc(bank_out[g % NB], 1)

        @block.tensor
        def _(pe):
            with pe.Fori(0, B) as b:
                for hf in range(NCH):
                    seen = set()
                    for g, k, t in tiles(hf):
                        what, s = jobs[k][:2]
                        if t == 0:
                            pe.wait_ge(w_ready, k + 1)
                        if s not in seen:
                            pe.wait_ge(lo_ready[s], b * NCH + hf + 1)
                            seen.add(s)
                        pe.wait_ge(bank_out[g % NB], b * ROUNDS + g // NB)
                        n = 0
                        for kt in range(KT):
                            for x, w in ((s_hi, w_hi), (s_hi, w_lo), (s_lo, w_hi)):
                                if what == "v":
                                    left, right = x[s][:, hf, kt, t * P:(t + 1) * P], w[k][:, kt, :]
                                else:
                                    left, right = w[k][:, kt, t * P:(t + 1) * P], x[s][:, hf, kt, :]
                                last = nc.tensor.matmul(bank[:, g % NB, :], left, right, start=(n == 0),
                                                        stop=(n == 3 * KT - 1))
                                n += 1
                        last.then_inc(tile_ready, 1)


RING = 4
SBANKS, TBANKS = 2, 2
PROBS = 8


def attend(nc, tag, q, k, v, att, sums, mask=None):
    causal = mask is None
    SPB = RING if causal else 2 * PAIRS
    TURNS = NSTEP // SPB
    ROWS = 3 * DH

    order = [t for pair in zip(range(KB - 1, -1, -1), range(KB // 2)) for t in pair]
    s_units = [(h, t, (t + 1) * P if causal else S) for h in range(2) for t in order]
    t_pairs = [(hf, j, q0, (hf + 1) * CH - q0) for hf in range(NCH) for j in range(KB)
               for q0 in [max(hf * CH, j * P) if causal else hf * CH] if q0 < (hf + 1) * CH]
    NS, NP = len(s_units), len(t_pairs)
    NT = 2 * NP
    assert NS == 2 * KB and KB % SBANKS == 0 and NT % PROBS == 0 and NP % 2 == 0
    last_of_half = [max(p for p, x in enumerate(t_pairs) if x[0] == hf) for hf in range(NCH)]
    first_of_half = [min(p for p, x in enumerate(t_pairs) if x[0] == hf) for hf in range(NCH)]
    EXPS0 = TBANKS
    USED0 = NP
    LOADS = 2 * ROWS // DH * 16

    with ExitStack() as ctx:
        m = Places(nc, ctx, tag)
        qs = m.sb("qs", [P, RING, 2, S], F32R)
        ks = m.sb("ks", [P, RING, 2, S], F32R)
        vs = m.sb("vs", [P, 2, KB, 2, 2 * DH])
        probs = m.sb("probs", [P, PROBS, CH])
        att_sb = m.sb("att_sb", [P, 2, NCH, CH])
        row_max = m.sb("row_max", [P, 2, 2 * KB])
        neg_max = m.sb("neg_max", [2 * KB, P], F32R)
        ident = m.sb("ident", [P, P])
        identb = m.sb("identb", [P, P], BF16)
        if causal:
            above = m.sb("above", [P, P], BF16)
        else:
            addend = m.sb("addend", [P, 2, KB, S], BF16)
            flag = m.sb("flag", [1, 1], I32)
        s_bank = m.ps("s_bank", [P, SBANKS, S])
        t_bank = m.ps("t_bank", [P, TBANKS, CH])
        acc = m.ps("acc", [P, NCH, CH])
        consts = m.sem("consts")
        ones_ready = m.sem("ones_ready")
        qk_loaded = m.sems("qk_loaded", RING)
        v_loaded = m.sems("v_loaded", 2)
        mask_loaded = m.sems("mask_loaded", 2)
        flag_loaded = m.sem("flag_loaded")
        s_ready = m.sem("s_ready")
        s_free = m.sems("s_free", SBANKS)
        max_turned = m.sem("max_turned")
        neg_ready = m.sem("neg_ready")
        neg_loaded = m.sem("neg_loaded")
        t_ready = m.sem("t_ready")
        exps = m.sem("exps")
        used = m.sem("used")
        att_out = m.sems("att_out", NCH)
        att_stored = m.sems("att_stored", 2)
        block = m.block()

        def ring_uses(i, r):
            return i * (SPB // RING) + r // RING

        def maxima_schedule(i, r):
            return [(r + 1, s) for s in range(KB, NS)] + [(r + 2, 0), (r + 1, "turn")] + [(r + 2, s) for s in range(1, KB)]

        FIRST = [(0, s) for s in range(NS)] + [(1, 0), (0, "turn")] + [(1, s) for s in range(1, KB)]

        @block.sync
        def _(sp):
            def load_qk(i, r):
                n = (i * SPB + r) % NSTEP
                rows = bass.ds(n * 2 * DH, 2 * DH)
                for to, parts in ((qs, (0, 1, 0)), (ks, (0, 0, 1))):
                    src = q if to is qs else k
                    for j, part in enumerate(parts):
                        sp.dma_start(to[j * DH:(j + 1) * DH, r % RING, :, :].bitcast(FP32),
                                     src[part][rows, :].rearrange("(h d) n -> d h n", h=2)
                                     ).then_inc(qk_loaded[r % RING], 16)

            def load_v(i, r):
                n = (i * SPB + r) % NSTEP
                for h in range(2):
                    sp.dma_start(vs[:, r % 2, :, h, 0:DH],
                                 v[bass.ds(n, 1), :, h * DH:(h + 1) * DH].rearrange("a (j p) d -> p (a j) d", p=P)
                                 ).then_inc(v_loaded[r % 2], 16)

            def put_maxima(i, r):
                sp.wait_ge(neg_ready, i * SPB + r + 1)
                sp.dma_start(qs[ROWS:ROWS + 1, r % RING, :, :].bitcast(FP32).rearrange("a h (t n) -> a (h t) n", n=P),
                             neg_max[:, :].bitcast(FP32)).then_inc(neg_loaded, 16)

            def load_mask(b, place):
                sp.dma_start(addend[:, place, :, :], mask[0][bass.ds(b * KB, KB), :, :].rearrange("t p n -> p t n")
                             ).then_inc(mask_loaded[place], 16)

            load_qk(0, 0)
            load_qk(0, 1)
            load_v(0, 0)
            if not causal:
                sp.dma_start(flag[:, :], mask[1]).then_inc(flag_loaded, 16)
                load_mask(0, 0)
            load_qk(0, 2)
            put_maxima(0, 0)
            with sp.Fori(0, TURNS) as i:
                for r in range(SPB):
                    n = i * SPB + r
                    sp.wait_ge(used, USED0 + n * NP)
                    load_qk(i, r + 3)
                    load_v(i, r + 1)
                    if not causal and r % PAIRS == 0:
                        load_mask((i * (SPB // PAIRS) + r // PAIRS + 1) % B, (r // PAIRS + 1) % 2)
                    put_maxima(i, r + 1)
                    for hf in range(NCH):
                        sp.wait_ge(att_out[hf], n + 1 + hf)
                    for h in range(2):
                        at = 2 * h * DH
                        sp.dma_start(att[bass.ds((n * 2 + h) * DH, DH), :].rearrange("d (c n) -> d c n", c=NCH),
                                     att_sb[at:at + DH, r % 2, :, :]).then_inc(att_stored[r % 2], 16)
                        sp.dma_start(sums[bass.ds(n * 2 + h, 1), :].rearrange("d (c n) -> d c n", c=NCH),
                                     att_sb[at + DH:at + DH + 1, r % 2, :, :]).then_inc(att_stored[r % 2], 16)
            for r in range(RING):
                sp.wait_ge(qk_loaded[r], LOADS * (NSTEP // RING + (r < 3)))
            sp.wait_ge(v_loaded[0], 32 * (NSTEP // 2 + 1))
            sp.wait_ge(neg_loaded, 16 * (NSTEP + 1))
            if not causal:
                sp.wait_ge(flag_loaded, 16)
                sp.wait_ge(mask_loaded[0], 16 * (B // 2 + 1))
                sp.wait_ge(mask_loaded[1], 16 * (B // 2))
            for x in range(2):
                sp.wait_ge(att_stored[x], 64 * (NSTEP // 2))

        @block.gpsimd
        def _(pool):
            pool.memset(ident[:, :], 0.0).then_inc(consts, 1)
            pool.memset(identb[:, :], 0.0).then_inc(consts, 1)
            pool.wait_ge(consts, 2)
            for x in (ident, identb):
                pool.affine_select(out=x[:, :], in_=x[:, :], compare_op=ALU.not_equal, fill=1.0, base=0,
                                   pattern=[[-1, P]], channel_multiplier=1).then_inc(consts, 1)
            if causal:
                pool.memset(above[:, :], 0.0).then_inc(consts, 1)
                pool.wait_ge(consts, 5)
                pool.affine_select(out=above[:, :], in_=above[:, :], compare_op=ALU.is_ge, fill=-BIG, base=0,
                                   pattern=[[-1, P]], channel_multiplier=1).then_inc(consts, 1)

        @block.scalar
        def _(act):
            def copy_out(place, hf):
                nc.scalar.activation(att_sb[:, place, hf, :], acc[:, hf, :], ACT.Copy).then_inc(att_out[hf], 1)

            act.wait_ge(ones_ready, 3)
            with act.Fori(0, TURNS) as i:
                for r in range(SPB):
                    n = i * SPB + r
                    for u in range(NT):
                        if u == 4:
                            act.wait_ge(used, USED0 + n * NP)
                            copy_out((r - 1) % 2, 1)
                        if u == 2 * last_of_half[0] + 6:
                            act.wait_ge(used, USED0 + n * NP + last_of_half[0] + 1)
                            act.wait_ge(att_stored[r % 2], (i * (SPB // 2) + r // 2) * 64)
                            copy_out(r % 2, 0)
                        w = t_pairs[u // 2][3]
                        act.wait_ge(t_ready, n * NT + u + 1)
                        act.wait_ge(used, USED0 + n * NP + (u - PROBS) // 2 + 1)
                        nc.scalar.activation(probs[:, u % PROBS, 0:w], t_bank[:, u % TBANKS, 0:w], ACT.Exp, scale=SCALE
                                             ).then_inc(exps, 1)
            act.wait_ge(used, USED0 + NSTEP * NP)
            copy_out(1, 1)

        @block.vector
        def _(dve):
            dve.memset(vs[:, :, :, :, DH:2 * DH], 1.0).then_inc(ones_ready, 1)
            dve.memset(ks[ROWS:ROWS + 1, :, :, :].bitcast(FP32), 1.0).then_inc(ones_ready, 1)
            dve.memset(acc[:, 1, :], 0.0).then_inc(ones_ready, 1)

            def maxima(i, r, s):
                n = i * SPB + r
                if s == "turn":
                    dve.wait_ge(max_turned, n + 1)
                    dve.wait_ge(neg_loaded, n * 16)
                    nc.vector.tensor_scalar(neg_max[:, :], s_bank[0:2 * KB, 1, 0:P], FLOOR, -1.0, ALU.max, ALU.mult
                                            ).then_inc(neg_ready, 1)
                    return
                h, t, w = s_units[s]
                dve.wait_ge(s_ready, n * NS + s + 1)
                nc.vector.tensor_reduce(row_max[:, r % 2, h * KB + t:h * KB + t + 1], s_bank[:, s % SBANKS, 0:w],
                                        AX.X, ALU.max).then_inc(s_free[s % SBANKS], 1)

            for r, s in FIRST:
                maxima(0, r, s)
            with dve.Fori(0, TURNS) as i:
                for r in range(SPB):
                    for x, s in maxima_schedule(i, r):
                        maxima(i, x, s)

        @block.tensor
        def _(pe):
            pe.wait_ge(consts, 6 if causal else 4)
            pe.wait_ge(ones_ready, 3)
            pe.sem_inc(exps, EXPS0)
            pe.sem_inc(used, USED0)

            def add_mask(to, left, right):
                return nc.tensor.matmul(to, left, right, start=False, stop=True, skip_group_check=True)

            def by_query(i, r, s, masked):
                n = i * SPB + r
                if s == "turn":
                    for x in range(SBANKS):
                        pe.wait_ge(s_free[x], (n + 1) * (NS // SBANKS))
                    nc.tensor.transpose(s_bank[0:2 * KB, 1, 0:P], row_max[:, r % 2, :], ident[:, :]).then_inc(max_turned, 1)
                    return
                h, t, w = s_units[s]
                if s == 0:
                    pe.wait_ge(qk_loaded[r % RING], (ring_uses(i, r) + 1) * LOADS)
                    if masked and r % PAIRS == 0:
                        pe.wait_ge(mask_loaded[r // PAIRS % 2], (i + r // SPB) * 16 + 16)
                pe.wait_ge(s_free[s % SBANKS], n * (NS // SBANKS) + s // SBANKS)
                if s == 1:
                    pe.wait_ge(neg_ready, n)
                to = s_bank[:, s % SBANKS, :]
                for k0 in range(0, w, CH):
                    k1 = min(k0 + CH, w)
                    last = nc.tensor.matmul(to[:, k0:k1], qs[0:ROWS, r % RING, h, t * P:(t + 1) * P],
                                            ks[0:ROWS, r % RING, h, k0:k1], start=True, stop=True)
                    if masked:
                        last = add_mask(to[:, k0:k1], identb[:, :], addend[:, r // PAIRS % 2, t, k0:k1])
                if causal:
                    last = add_mask(to[:, t * P:(t + 1) * P], identb[:, :], above[:, :])
                last.then_inc(s_ready, 1)

            def by_key(i, r, p, masked):
                n, (hf, j, q0, w) = i * SPB + r, t_pairs[p]
                if p == 0:
                    pe.wait_ge(neg_loaded, n * 16 + 16)
                for h in range(2):
                    u = 2 * p + h
                    pe.wait_ge(exps, EXPS0 + n * NT + u - TBANKS + 1)
                    to = t_bank[:, u % TBANKS, :]
                    last = nc.tensor.matmul(to[:, 0:w], ks[0:ROWS + 1, r % RING, h, j * P:(j + 1) * P],
                                            qs[0:ROWS + 1, r % RING, h, q0:q0 + w], start=True, stop=True)
                    if causal and j * P >= hf * CH:
                        last = add_mask(to[:, 0:P], above[:, :], identb[:, :])
                    for x in range(w // P if masked else 0):
                        last = add_mask(to[:, x * P:(x + 1) * P], addend[:, r // PAIRS % 2, q0 // P + x, j * P:(j + 1) * P],
                                        identb[:, :])
                    last.then_inc(t_ready, 1)

            def values(i, r, p):
                n, (hf, j, q0, w) = i * SPB + r, t_pairs[p]
                if p == 0:
                    pe.wait_ge(v_loaded[r % 2], (i * (SPB // 2) + r // 2 + 1) * 32)
                if p == first_of_half[hf]:
                    pe.wait_ge(att_out[hf], n + hf)
                pe.wait_ge(exps, EXPS0 + n * NT + 2 * p + 2)
                at = q0 - hf * CH
                for h in range(2):
                    last = nc.tensor.matmul(acc[2 * DH * h:2 * DH * (h + 1), hf, at:at + w], vs[:, r % 2, j, h, :],
                                            probs[:, (2 * p + h) % PROBS, 0:w], start=j == 0, stop=True,
                                            skip_group_check=True)
                last.then_inc(used, 1)

            def steps(masked):
                for r, s in FIRST:
                    by_query(0, r, s, masked)
                by_key(0, 0, 0, masked)
                with pe.Fori(0, TURNS) as i:
                    for r in range(SPB):
                        todo, asked = maxima_schedule(i, r), 0
                        for p in range(NP):
                            while asked * NP < (p + 1) * (NS + 1) and asked < NS + 1:
                                x, s = todo[asked]
                                by_query(i, x, s, masked)
                                asked += 1
                            by_key(i, r + (p + 1) // NP, (p + 1) % NP, masked)
                            values(i, r, p)

            if causal:
                steps(False)
            else:
                pe.wait_ge(flag_loaded, 16)
                any_masked = pe.value_load(flag[0:1, 0:1])
                with pe.If(any_masked > 0):
                    steps(True)
                with pe.Else():
                    steps(False)


def feed_forward(nc, tag, att, sums, inverse, x, w, out):
    FT = FF // P
    PIECES = 2
    PT = CH // PIECES
    WP = FF // D
    NCHUNK = B * NCH
    START = [0, 8]
    SUMMED, HIGH, MEAN, CENTRED, SQUARED, VAR, ROOT, SCALED, DONE = 0, 0, 2, 2, 3, 4, 4, 5, 6

    def following(b, hf):
        return (b, hf + 1) if hf + 1 < NCH else ((b + 1) % B, 0)

    with ExitStack() as ctx:
        m = Places(nc, ctx, tag)
        w1_hi, w1_lo = (m.sb(f"w1_{x}", [P, KT, FF], F32R) for x in ("hi", "lo"))
        w2_hi, w2_lo = (m.sb(f"w2_{x}", [P, FT, D], F32R) for x in ("hi", "lo"))
        w_raw = m.sb("w_raw", [P, KT, D])
        y_hi, y_lo = (m.sb(f"y_{x}", [P, NCH, KT, CH], F32R) for x in ("hi", "lo"))
        h = m.sb("h", [P, KT, PT])
        aux = m.sb("aux", [P, KT, PT])
        xin = m.sb("xin", [P, KT, PT])
        p_hi, p_lo = (m.sb(f"p_{x}", [P, KT, PT], F32R) for x in ("hi", "lo"))
        dev = m.sb("dev", [P, PT])
        gelu = m.sb("gelu", [P, 2, CH])
        packed = gelu[:, 0, :]
        assert CH == B * H * S // P
        g_hi, g_lo = (m.sb(f"g_{x}", [P, 2, CH], F32R) for x in ("hi", "lo"))
        done = m.sb("done", [P, 2, CH])
        mean_w = m.sb("mean_w", [P, P], F32R)
        mean_f = m.sb("mean_f", [P, P])
        eps = m.sb("eps", [P, 1])
        b1 = m.sb("b1", [P, FT])
        b2, gain, shift = (m.sb(x, [P, KT]) for x in ("b2", "gain", "shift"))
        acc = m.ps("acc", [P, KT, CH])
        hid = m.ps("hid", [P, 2, CH])
        stat = m.ps("stat", [P, 2, CH])
        w_loaded = m.sem("w_loaded")
        w_hi_ready = m.sem("w_hi_ready")
        w_ready = m.sem("w_ready")
        vec_loaded = m.sem("vec_loaded")
        consts = m.sem("consts")
        packed_loaded = m.sem("packed_loaded")
        packed_ready = m.sem("packed_ready")
        packed_stored = m.sem("packed_stored")
        x_loaded = m.sem("x_loaded")
        inverse_loaded = m.sem("inverse_loaded")
        att_loaded = m.sem("att_loaded")
        ln_dve = m.sem("ln_dve")
        ln_hi = m.sem("ln_hi")
        ln_lo = m.sem("ln_lo")
        ln_stat = m.sem("ln_stat")
        squared = m.sem("squared")
        rooted = m.sem("rooted")
        y_hi_ready = m.sem("y_hi_ready")
        y_ready = m.sem("y_ready")
        hid_ready = m.sem("hid_ready")
        gelu_ready = m.sems("gelu_ready", 2)
        g_hi_ready = m.sem("g_hi_ready")
        g_ready = m.sems("g_ready", 2)
        g_used = m.sems("g_used", 2)
        acc_out = m.sem("acc_out")
        x_ready = m.sem("x_ready")
        stored = m.sems("stored", 2)
        block = m.block()
        DVE_STEPS = 2 + 1 + 2 + KT

        def at(slot, step):
            return [p for p in range(PIECES) if START[p] + step == slot]

        @block.sync
        def _(sp):
            def load_x(b, c):
                sp.dma_start(xin[:, :, :], x[bass.ds(b * D, D), c].rearrange("(k p) n -> p k n", p=P)).then_inc(x_loaded, 16)

            def load_inverse(b, c):
                for to, src in by_head(inverse, b, c, aux):
                    sp.dma_start(to, src).then_inc(inverse_loaded, 16)

            def load_att(b, c):
                sp.dma_start(h[:, :, :], att[bass.ds(b * D, D), c].rearrange("(k p) n -> p k n", p=P)
                             ).then_inc(att_loaded, 16)

            def load_after(q, b, hf, p):
                c = slice(hf * CH + p * PT, hf * CH + (p + 1) * PT)
                sp.wait_ge(ln_dve, q * DVE_STEPS + 2)
                load_x(b, c)
                sp.wait_ge(ln_lo, 2 * q + 2)
                load_inverse(b, c)
                sp.wait_ge(y_ready, q + 1)
                load_att(b, c)

            lines = "r (c n) -> (r c) n"
            sp.dma_start(packed, sums.rearrange(lines, c=P // (B * H))).then_inc(packed_loaded, 16)
            for to, src in ((b1, w["b1"]), (b2, w["b2"]), (gain, w["g"]), (shift, w["beta"])):
                sp.dma_start(to[:, :], src).then_inc(vec_loaded, 16)
            load_x(0, slice(0, PT))
            load_att(0, slice(0, PT))
            sp.wait_ge(packed_ready, 1)
            sp.dma_start(inverse.rearrange(lines, c=P // (B * H)), packed).then_inc(packed_stored, 16)
            sp.wait_ge(packed_stored, 16)
            load_inverse(0, slice(0, PT))
            k = 0
            for c in range(WP):
                for src in (w["W1"].rearrange("(k p) n -> p k n", p=P)[:, :, c * D:(c + 1) * D],
                            w["W2"].rearrange("(k p) n -> p k n", p=P)[:, c * KT:(c + 1) * KT, :]):
                    if k:
                        sp.wait_ge(w_ready, k)
                    sp.dma_start(w_raw[:, :, :], src).then_inc(w_loaded, 16)
                    k += 1
                    if k == 3:
                        load_after(0, 0, 0, 1)
                    if k == 6:
                        load_after(1, *following(0, 0), 0)
            with sp.Fori(0, B) as b:
                for hf in range(NCH):
                    n = b * NCH + hf
                    load_after(PIECES * (n + 1), *following(b, hf), 1)
                    load_after(PIECES * (n + 1) + 1, (b + 1) % B, hf, 0)
                    for t in range(KT):
                        sp.wait_ge(x_ready, n * KT + t + 1)
                        sp.nop(nofuse=True)
                        sp.dma_start(out[bass.ds(b * D + t * P, P), hf * CH:(hf + 1) * CH], done[:, t % 2, :]
                                     ).then_inc(stored[t % 2], 16)
            for n in range(2):
                sp.wait_ge(stored[n], 16 * NCHUNK * KT // 2)
            loads = PIECES * (NCHUNK + 1) + 1
            sp.wait_ge(x_loaded, 16 * loads)
            sp.wait_ge(inverse_loaded, P // DH * 16 * loads)
            sp.wait_ge(att_loaded, 16 * loads)

        @block.gpsimd
        def _(pool):
            def low_parts(hf, p, q):
                for k, src in ((0, h), (1, aux)):
                    pool.wait_ge(ln_hi, 2 * q + k + 1)
                    nc.gpsimd.tensor_tensor(p_lo[:, :, :], src[:, :, :], p_hi[:, :, :].bitcast(FP32), ALU.subtract
                                            ).then_inc(ln_lo, 1)
                pool.wait_ge(y_hi_ready, q + 1)
                nc.gpsimd.tensor_tensor(y_lo[:, hf, :, p * PT:(p + 1) * PT], h[:, :, :],
                                        y_hi[:, hf, :, p * PT:(p + 1) * PT].bitcast(FP32), ALU.subtract
                                        ).then_inc(y_ready, 1)

            for p in range(PIECES):
                low_parts(0, p, p)
            with pool.Fori(0, B) as b:
                for hf in range(NCH):
                    for p in range(PIECES):
                        low_parts((hf + 1) % NCH, p, PIECES * (b * NCH + hf + 1) + p)

        @block.scalar
        def _(act):
            def high(hf, p, q):
                act.wait_ge(ln_dve, q * DVE_STEPS + 2)
                nc.scalar.activation(p_hi[:, :, :], h[:, :, :], ACT.Copy).then_inc(ln_hi, 1)

            def square(hf, p, q):
                act.wait_ge(ln_dve, q * DVE_STEPS + 3)
                nc.scalar.activation(aux[:, :, :], h[:, :, :], ACT.Square).then_inc(squared, 1)
                act.wait_ge(squared, q + 1)
                nc.scalar.activation(p_hi[:, :, :], aux[:, :, :], ACT.Copy).then_inc(ln_hi, 1)

            def root(hf, p, q):
                act.wait_ge(ln_stat, 2 * q + 2)
                nc.scalar.activation(dev[:, :], stat[:, 1, 0:PT], ACT.Sqrt, bias=eps[:, :]).then_inc(rooted, 1)

            def y_high(hf, p, q, chunks):
                act.wait_ge(ln_dve, (q + 1) * DVE_STEPS)
                if chunks is not None:
                    act.wait_ge(x_ready, chunks * KT)
                nc.scalar.activation(y_hi[:, hf, :, p * PT:(p + 1) * PT], h[:, :, :], ACT.Copy).then_inc(y_hi_ready, 1)

            act.wait_ge(vec_loaded, 64)
            act.wait_ge(consts, 3)
            for p in range(PIECES):
                high(0, p, p)
                square(0, p, p)
                root(0, p, p)
                y_high(0, p, p, None)
            with act.Fori(0, B) as b:
                for hf in range(NCH):
                    n = b * NCH + hf
                    nxt = (hf + 1) % NCH
                    for f in range(FT):
                        q = PIECES * (n + 1)
                        for p in at(f, HIGH):
                            high(nxt, p, q + p)
                        for p in at(f, SQUARED):
                            square(nxt, p, q + p)
                        for p in at(f, ROOT):
                            root(nxt, p, q + p)
                        for p in at(f, DONE):
                            y_high(nxt, p, q + p, n)
                        act.wait_ge(hid_ready, n * FT + f + 1)
                        act.wait_ge(g_ready[f % 2], n * (FT // 2) + f // 2)
                        nc.scalar.activation(gelu[:, f % 2, :], hid[:, f % 2, :], ACT.Gelu, bias=b1[:, f:f + 1]
                                             ).then_inc(gelu_ready[f % 2], 1)

        @block.vector
        def _(dve):
            def spread(v):
                return v.unsqueeze(1).to_broadcast([P, KT, PT])

            def summed(q):
                s = q * DVE_STEPS
                dve.wait_ge(att_loaded, (q + 1) * 16)
                dve.wait_ge(inverse_loaded, (q + 1) * (P // DH * 16))
                dve.wait_ge(x_loaded, (q + 1) * 16)
                nc.vector.tensor_tensor(h[:, :, :], h[:, :, :], aux[:, :, :], ALU.mult).then_inc(ln_dve, 1)
                dve.wait_ge(ln_dve, s + 1)
                nc.vector.tensor_tensor(h[:, :, :], h[:, :, :], xin[:, :, :], ALU.add).then_inc(ln_dve, 1)

            def centred(q):
                dve.wait_ge(ln_stat, 2 * q + 1)
                nc.vector.tensor_tensor(h[:, :, :], h[:, :, :], spread(stat[:, 0, 0:PT]), ALU.subtract).then_inc(ln_dve, 1)

            def scaled(q):
                s = q * DVE_STEPS + 3
                dve.wait_ge(rooted, q + 1)
                nc.vector.reciprocal(dev[:, :], dev[:, :]).then_inc(ln_dve, 1)
                dve.wait_ge(ln_dve, s + 1)
                nc.vector.tensor_tensor(h[:, :, :], h[:, :, :], spread(dev[:, :]), ALU.mult).then_inc(ln_dve, 1)
                dve.wait_ge(ln_dve, s + 2)
                for k in range(KT):
                    nc.vector.tensor_scalar(h[:, k, :], h[:, k, :], gain[:, k:k + 1], shift[:, k:k + 1], ALU.mult, ALU.add
                                            ).then_inc(ln_dve, 1)

            dve.wait_ge(packed_loaded, 16)
            nc.vector.reciprocal(packed, packed).then_inc(packed_ready, 1)
            dve.memset(mean_f[:, :], 1.0 / D).then_inc(consts, 1)
            dve.memset(eps[:, :], LN_EPS).then_inc(consts, 1)
            dve.wait_ge(consts, 2)
            nc.vector.tensor_copy(mean_w[:, :], mean_f[:, :]).then_inc(consts, 1)
            dve.wait_ge(vec_loaded, 64)

            def split_weights(k):
                to_hi, to_lo = ((w1_hi, w1_lo), (w2_hi, w2_lo))[k % 2]
                c = k // 2
                part = (slice(None), slice(None), slice(c * D, (c + 1) * D)) if k % 2 == 0 else (
                    slice(None), slice(c * KT, (c + 1) * KT), slice(None))
                dve.wait_ge(w_loaded, 16 * (k + 1))
                nc.vector.tensor_copy(to_hi[part], w_raw[:, :, :]).then_inc(w_hi_ready, 1)
                dve.wait_ge(w_hi_ready, k + 1)
                nc.vector.tensor_tensor(to_lo[part], w_raw[:, :, :], to_hi[part].bitcast(FP32), ALU.subtract
                                        ).then_inc(w_ready, 1)

            for p in range(PIECES):
                summed(p)
                split_weights(3 * p)
                centred(p)
                split_weights(3 * p + 1)
                split_weights(3 * p + 2)
                scaled(p)
            for k in range(3 * PIECES, 2 * WP):
                split_weights(k)
            with dve.Fori(0, B) as b:
                for hf in range(NCH):
                    n = b * NCH + hf
                    q = PIECES * (n + 1)
                    for f in range(FT):
                        for p in at(f, SUMMED):
                            summed(q + p)
                        for p in at(f, CENTRED):
                            centred(q + p)
                        for p in at(f, SCALED):
                            scaled(q + p)
                        s = f % 2
                        dve.wait_ge(gelu_ready[s], n * (FT // 2) + f // 2 + 1)
                        dve.wait_ge(g_used[s], n * (FT // 2) + f // 2)
                        nc.vector.tensor_copy(g_hi[:, s, :], gelu[:, s, :]).then_inc(g_hi_ready, 1)
                        dve.wait_ge(g_hi_ready, n * FT + f + 1)
                        nc.vector.tensor_tensor(g_lo[:, s, :], gelu[:, s, :], g_hi[:, s, :].bitcast(FP32), ALU.subtract
                                                ).then_inc(g_ready[s], 1)
                    for t in range(KT):
                        dve.wait_ge(g_used[1], (n + 1) * (FT // 2))
                        dve.wait_ge(stored[t % 2], n * (KT // 2) * 16 + t // 2 * 16)
                        nc.vector.scalar_tensor_tensor(done[:, t % 2, :], acc[:, t, :], b2[:, t:t + 1],
                                                       y_hi[:, hf, t, :].bitcast(FP32), ALU.add, ALU.add).then_inc(acc_out, 1)
                        dve.wait_ge(acc_out, n * KT + t + 1)
                        nc.vector.tensor_tensor(done[:, t % 2, :], done[:, t % 2, :], y_lo[:, hf, t, :].bitcast(FP32),
                                                ALU.add).then_inc(x_ready, 1)

        @block.tensor
        def _(pe):
            def statistic(k, q):
                pe.wait_ge(ln_lo, 2 * q + k + 1)
                n = 0
                for part in (p_hi, p_lo):
                    for t in range(KT):
                        last = nc.tensor.matmul(stat[:, k, 0:PT], mean_w[:, :], part[:, t, :], start=n == 0,
                                                stop=n == 2 * KT - 1)
                        n += 1
                last.then_inc(ln_stat, 1)

            def product(to, left, right, first, last_one):
                n, count = 0, 3 * len(left)
                for (l_hi, l_lo), (r_hi, r_lo) in zip(left, right):
                    for l, r in ((l_hi, r_hi), (l_lo, r_hi), (l_hi, r_lo)):
                        last = nc.tensor.matmul(to, l, r, start=first and n == 0, stop=last_one and n == count - 1)
                        n += 1
                return last

            def hidden(hf, n, f):
                pe.wait_ge(w_ready, 2 * (f // KT) + 1)
                if f == 0:
                    pe.wait_ge(y_ready, PIECES * (n + 1))
                pe.wait_ge(gelu_ready[f % 2], n * (FT // 2) + f // 2)
                c = slice(f * P, (f + 1) * P)
                product(hid[:, f % 2, :], [(w1_hi[:, k, c], w1_lo[:, k, c]) for k in range(KT)],
                        [(y_hi[:, hf, k, :], y_lo[:, hf, k, :]) for k in range(KT)], True, True).then_inc(hid_ready, 1)

            def output(n, f):
                pe.wait_ge(w_ready, 2 * (f // KT) + 2)
                pe.wait_ge(g_ready[f % 2], n * (FT // 2) + f // 2 + 1)
                for t in range(KT):
                    if f == 0:
                        pe.wait_ge(acc_out, n * KT)
                    c = slice(t * P, (t + 1) * P)
                    last = product(acc[:, t, :], [(w2_hi[:, f, c], w2_lo[:, f, c])], [(g_hi[:, f % 2, :], g_lo[:, f % 2, :])],
                                   f == 0, f == FT - 1)
                last.then_inc(g_used[f % 2], 1)

            pe.wait_ge(consts, 3)
            for p in range(PIECES):
                statistic(0, p)
                statistic(1, p)
            with pe.Fori(0, B) as b:
                for hf in range(NCH):
                    n = b * NCH + hf
                    hidden(hf, n, 0)
                    for f in range(FT):
                        for p in at(f, MEAN):
                            statistic(0, PIECES * (n + 1) + p)
                        for p in at(f, VAR):
                            statistic(1, PIECES * (n + 1) + p)
                        if f + 1 < FT:
                            hidden(hf, n, f + 1)
                        output(n, f)


def program(nc, a, out, debug=None):
    def dram(name, shape, dtype=FP32):
        return nc.dram_tensor(f"scratch_{name}", shape, dtype, kind="Internal").ap()

    trig = dram("trig", [2, P, B * S])
    maskadd = dram("maskadd", [B * KB, P, S], BF16)
    anymask = dram("anymask", [1, 1], I32)
    q0h, q0l, k0h, k0l, k1h, k1l, q1h, q1l = (dram(n, [B * D, S]) for n in
                                              ("q0h", "q0l", "k0h", "k0l", "k1h", "k1l", "q1h", "q1l"))
    v0, v1 = (dram(n, [NSTEP, S, 2 * DH]) for n in ("v0", "v1"))
    prepare_tables(nc, "tab", a["tokens"], a["trig"], a["mask"], trig, maskadd, anymask)
    project(nc, "proj", [(a["x"], None), (a["ctx"], None)], [
        ("t", 0, a["Wq0"], a["bq0"], (q0h, q0l)),
        ("r", 1, a["Wk1"], None, (k1h, k1l)),
        ("t", 1, a["Wk0"], a["bk0"], (k0h, k0l)),
        ("v", 1, a["Wv0"], a["bv0"], (v0,)),
        ("v", 1, a["Wv1"], a["bv1"], (v1,)),
    ], trig)
    att0, att1 = (dram(n, [B * D, S]) for n in ("att0", "att1"))
    sum0, sum1, inv0, inv1 = (dram(n, [B * H, S]) for n in ("sum0", "sum1", "inv0", "inv1"))
    attend(nc, "att0", (q0h, q0l), (k0h, k0l), v0, att0, sum0)
    x1 = dram("x1", [B * D, S])
    feed_forward(nc, "ffn", att0, sum0, inv0, a["x"], a, x1)
    project(nc, "q1", [(x1, None)], [("r", 0, a["Wq1"], a["bq1"], (q1h, q1l))], trig)
    attend(nc, "att1", (q1h, q1l), (k1h, k1l), v1, att1, sum1, (maskadd, anymask))
    project(nc, "out", [(att1, (sum1, inv1))], [("o", 0, a["Wo"], a["bo"], (out, x1))])


def kernel(**inputs):
    import concourse.bacc as bacc
    from concourse.bass_utils import run_bass_kernel_spmd

    f = {k: np.asarray(v) for k, v in inputs.items()}

    def turned(v):
        return np.ascontiguousarray(np.swapaxes(v, -1, -2))

    def columns(v):
        return np.ascontiguousarray(v.reshape(-1, P).T)

    def rows(v):
        return np.ascontiguousarray(np.broadcast_to(v, (P, v.size)))

    def halves(v):
        return np.ascontiguousarray(v.reshape(-1, H // 8, 8, 2, DH // 2).transpose(0, 1, 3, 2, 4).reshape(v.shape))

    inv_freq = np.float32(1.0) / np.power(np.float32(10000.0), np.arange(0, DH, 2, dtype=np.float32) / np.float32(DH))
    angle = np.arange(MAX_POS, dtype=np.float32)[:, None] * inv_freq[None]
    trig = np.concatenate([np.tile(np.cos(angle), (1, 8)), np.tile(np.sin(angle), (1, 8))], axis=1).astype(np.float32)

    arrays = {
        "x": turned(f["x"]).reshape(B * D, S),
        "ctx": turned(f["ctx_1024"]).reshape(B * D, S),
        "tokens": np.ascontiguousarray(f["itok_BxS2_0_2047"].reshape(B * KB, P).T).view(np.uint32),
        "trig": trig,
        "mask": np.ascontiguousarray(f["mask_BxSxS2_bf0"]).reshape(B * KB, P, S),
        "Wq0": turned(f["L0_xattn_Wq"]), "bq0": columns(f["L0_xattn_bq"]),
        "Wk0": turned(f["L0_xattn_Wk"]), "bk0": columns(f["L0_xattn_bk"]),
        "Wv0": turned(f["L0_xattn_Wv"]), "bv0": rows(f["L0_xattn_bv"]),
        "W1": turned(f["L0_xattn_W1"]), "b1": columns(f["L0_xattn_b1"]),
        "W2": turned(f["L0_xattn_W2"]), "b2": columns(f["L0_xattn_b2"]),
        "g": columns(f["L0_xattn_ln_g"]), "beta": columns(f["L0_xattn_ln_b"]),
        "Wq1": halves(f["L1_xattn_q_w"]), "bq1": columns(halves(f["L1_xattn_q_b"])),
        "Wk1": halves(f["L1_xattn_k_w"]),
        "Wv1": np.ascontiguousarray(f["L1_xattn_v_w"]), "bv1": rows(f["L1_xattn_v_b"]),
        "Wo": np.ascontiguousarray(f["L1_xattn_proj_w"]), "bo": columns(f["L1_xattn_proj_b"]),
    }
    nc = bacc.Bacc("TRN2", target_bir_lowering=False, num_devices=1)
    a = {k: nc.dram_tensor(f"in_{k}", v.shape, mybir.dt.from_np(v.dtype), kind="ExternalInput").ap()
         for k, v in arrays.items()}
    out = nc.dram_tensor("out", (B * D, S), FP32, kind="ExternalOutput").ap()
    program(nc, a, out)
    r = run_bass_kernel_spmd(nc, [{f"in_{k}": v for k, v in arrays.items()}], core_ids=[0])
    return turned(np.asarray(r.results[0]["out"]).reshape(B, D, S))
```

```python
from contextlib import ExitStack

import numpy as np

import concourse.bass as bass
from concourse import mybir

FP32 = mybir.dt.float32
F32R = mybir.dt.float32r
BF16 = mybir.dt.bfloat16
U8 = mybir.dt.uint8
U32 = mybir.dt.uint32
I32 = mybir.dt.int32
ALU = mybir.AluOpType
ACT = mybir.ActivationFunctionType
AX = mybir.AxisListType

P = 128
B, S, D = 4, 1024, 512
H, DH = 16, 32
FF = 2048
MAX_POS = 1024
KT = D // P
CH = 512
NCH = S // CH
PAIRS = H // 2
NSTEP = B * PAIRS
KB = S // P
BIG = 1.0e30
FLOOR = -0.5 * BIG
SCALE = float(DH) ** -0.5
LN_EPS = 1e-5
STAGES = 4




class Places:

    def __init__(self, nc, ctx, tag):
        self.nc, self.ctx, self.tag = nc, ctx, tag
        self.handles = []

    def clear(self):
        self.nc.clear_and_free_semaphores(self.handles)
        self.nc.all_engine_barrier()

    def block(self):
        self.ctx.callback(self.clear)
        return self.ctx.enter_context(self.nc.Block())

    def sb(self, name, shape, dtype=FP32):
        return self.ctx.enter_context(self.nc.sbuf_tensor(f"{self.tag}_{name}", shape, dtype))

    def ps(self, name, shape):
        return self.ctx.enter_context(self.nc.psum_tensor(f"{self.tag}_{name}", shape, FP32))

    def sem(self, name):
        self.handles.append(self.nc.alloc_semaphore(f"{self.tag}_{name}"))
        return self.handles[-1]

    def sems(self, name, n):
        return [self.sem(f"{name}{i}") for i in range(n)]


def by_head(inverses, b, c, to):
    parts = P // DH
    heads = inverses[bass.ds(b * H, H), c].rearrange("(k j) n -> j k n", j=parts)
    return [(to[j * DH:(j + 1) * DH, :, :], heads[j].unsqueeze(0).to_broadcast([DH, KT, c.stop - c.start]))
            for j in range(parts)]


def project(nc, tag, sources, jobs, rope=None):
    NW, NS = len(jobs), len(sources)
    NTILE = KT * NW
    BODY = NCH * NTILE
    NB = 8 if rope is None else 4
    ROUNDS = BODY // NB
    TB = CH // P
    assert BODY % NB == 0 and BODY % STAGES == 0
    normed = sources[0][1] is not None
    rotary = [k for k, job in enumerate(jobs) if job[0] == "r"]
    residual = next((job[4][1] for job in jobs if job[0] == "o"), None)
    WPLACES = 3
    ROPE_OPS = 6
    ROPE_CHUNK = 2 * len(rotary) * ROPE_OPS
    COPIES = 2 if NS == 1 else 1

    def kind(g):
        return jobs[g % NTILE // KT][0]

    def tiles(hf):
        return [(hf * NTILE + k * KT + t, k, t) for k in range(NW) for t in range(KT)]

    def splits_before(g):
        return sum(kind(n) in "tr" for n in range(g))

    def pairs_before(g):
        return sum(kind(n) == "r" for n in range(g)) // 2

    def stores(slot, upto):
        return sum((32 if kind(n) in "tr" else 16) for n in range(slot, upto, STAGES))

    def chunk(b, x):
        return ((b + x // NCH) % B if x >= NCH else b), x % NCH

    def loads(b, x):
        return b * (NCH // COPIES) + x // COPIES + 1

    with ExitStack() as ctx:
        m = Places(nc, ctx, tag)
        w_raw = m.sb("w_raw", [P, WPLACES, D])
        w_hi = [m.sb(f"w_hi{k}", [P, KT, D], F32R) for k in range(NW)]
        w_lo = [m.sb(f"w_lo{k}", [P, KT, D], F32R) for k in range(NW)]
        raw = [m.sb(f"raw{s}", [P, COPIES, KT, CH]) for s in range(NS)]
        s_hi = [m.sb(f"s_hi{s}", [P, 2, KT, CH], F32R) for s in range(NS)]
        s_lo = [m.sb(f"s_lo{s}", [P, 2, KT, CH], F32R) for s in range(NS)]
        full = m.sb("full", [P, STAGES, CH])
        hi = m.sb("hi", [P, STAGES, CH], F32R)
        lo = m.sb("lo", [P, STAGES, CH], F32R)
        inverse = m.sb("inverse", [P, COPIES, KT, CH]) if normed else None
        packed = m.sb("packed", [P, B * H * S // P]) if normed else None
        trig = m.sb("trig", [P, COPIES, 2, CH]) if rotary else None
        turn = m.sb("turn", [P, 2, CH]) if rotary else None
        index = m.sb("index", [P, TB], U32) if rotary else None
        rows = m.sb("rows", [P, TB, 2, P]) if rotary else None
        ident = m.sb("ident", [P, P]) if rotary else None
        res = m.sb("res", [P, 2, KT, CH]) if residual is not None else None
        bias = {k: m.sb(f"bias{k}", [P, D] if job[0] == "v" else [P, KT])
                for k, job in enumerate(jobs) if job[3] is not None}
        bank = m.ps("bank", [P, NB, CH])
        trig_bank = m.ps("trig_bank", [P, 2, CH]) if rotary else None
        w_loaded = m.sems("w_loaded", WPLACES)
        w_hi_ready = m.sem("w_hi_ready")
        w_ready = m.sem("w_ready")
        bias_loaded = m.sem("bias_loaded")
        raw_loaded = [m.sems(f"raw{s}_loaded", COPIES) for s in range(NS)]
        packed_loaded = m.sem("packed_loaded")
        packed_ready = m.sem("packed_ready")
        packed_stored = m.sem("packed_stored")
        inverse_loaded = m.sems("inverse_loaded", COPIES)
        normed_ready = m.sem("normed_ready")
        hi_ready = m.sems("hi_ready", NS)
        lo_ready = m.sems("lo_ready", NS)
        ident_ready = m.sem("ident_ready")
        index_loaded = m.sem("index_loaded")
        rows_loaded = m.sem("rows_loaded")
        rows_turned = m.sem("rows_turned")
        trig_ready = m.sem("trig_ready")
        res_loaded = m.sems("res_loaded", NCH)
        tile_ready = m.sem("tile_ready")
        bank_out = m.sems("bank_out", NB)
        rope_done = m.sem("rope_done")
        tile_hi = m.sem("tile_hi")
        tile_split = m.sem("tile_split")
        stored = m.sems("stored", STAGES)
        block = m.block()

        def out_of_bank(b, g):
            return b * ROUNDS + (g // NB + 1)

        @block.sync
        def _(sp):
            for k, job in enumerate(jobs):
                for x in range(k * KT, (k + 1) * KT):
                    if x >= WPLACES:
                        sp.wait_ge(w_ready, x - WPLACES + 1)
                    sp.dma_start(w_raw[:, x % WPLACES, :], job[2][x % KT * P:(x % KT + 1) * P, :]
                                 ).then_inc(w_loaded[x % WPLACES], 16)
                if k in bias:
                    sp.dma_start(bias[k][:, :], job[3]).then_inc(bias_loaded, 16)
            with sp.Fori(0, B) as b:
                for hf in range(NCH):
                    c = slice(hf * CH, (hf + 1) * CH)
                    for g, k, t in tiles(hf):
                        what, outs, slot = jobs[k][0], jobs[k][4], g % STAGES
                        if what in "tr":
                            sp.wait_ge(tile_split, b * splits_before(BODY) + splits_before(g) + 1)
                            for part, dram in ((hi, outs[0]), (lo, outs[1])):
                                if what == "t":
                                    to = dram[bass.ds(b * D + t * P, P), c]
                                else:
                                    to = dram[bass.ds(b * D + (t // 2) * 2 * P, 2 * P), c].rearrange(
                                        "(h two s) n -> two h s n", two=2, s=DH // 2)[t % 2]
                                sp.dma_start(to, part[:, slot, :].bitcast(FP32)).then_inc(stored[slot], 16)
                            continue
                        sp.wait_ge(bank_out[g % NB], out_of_bank(b, g))
                        if what == "v":
                            rows = slice(hf * CH + t * P, hf * CH + (t + 1) * P)
                            to = outs[0][bass.ds(b * PAIRS, PAIRS), rows, :].rearrange("a p d -> p a d")
                            sp.dma_start(to, full[:, slot, :].rearrange("p (a d) -> p a d", a=PAIRS)
                                         ).then_inc(stored[slot], 16)
                        else:
                            sp.dma_start(outs[0][bass.ds(b * D + t * P, P), c], full[:, slot, :]
                                         ).then_inc(stored[slot], 16)
            for slot in range(STAGES):
                sp.wait_ge(stored[slot], B * stores(slot, BODY))

        @block.gpsimd
        def _(pool):
            def load(b, x):
                at, (batch, hf) = x % COPIES, chunk(b, x)
                c = slice(hf * CH, (hf + 1) * CH)
                for s, (raw_dram, sums_dram) in enumerate(sources):
                    if x >= COPIES:
                        pool.wait_ge(lo_ready[s], b * NCH + x - COPIES + 1)
                        pool.nop(nofuse=True)
                    pool.dma_start(raw[s][:, at, :, :], raw_dram[bass.ds(batch * D, D), c].rearrange(
                        "(k p) n -> p k n", p=P)).then_inc(raw_loaded[s][at], 16)
                    if normed:
                        for to, src in by_head(sums_dram[1], batch, c, inverse[:, at, :, :]):
                            pool.dma_start(to, src).then_inc(inverse_loaded[at], 16)

            def gather(b, x):
                batch, hf = chunk(b, x)
                if x:
                    pool.wait_ge(rows_turned, b * NCH + x)
                    pool.nop(nofuse=True)
                pool.dma_start(index[:, :], rope[0][:, bass.ds(batch * KB + hf * TB, TB)]).then_inc(index_loaded, 16)
                pool.wait_ge(index_loaded, (b * NCH + x + 1) * 16)
                pool.nop(nofuse=True)
                for t in range(TB):
                    pool.indirect_dma_start(out=rows[:, t, :, :].rearrange("p c n -> p (c n)"), out_offset=None,
                                            in_=rope[1][:, :],
                                            in_offset=bass.IndirectOffsetOnAxis(ap=index[:, t:t + 1], axis=0)
                                            ).then_inc(rows_loaded, 16)

            def low_parts(b, x):
                for s in range(NS):
                    pool.wait_ge(hi_ready[s], b * NCH + x + 1)
                    nc.gpsimd.tensor_tensor(s_lo[s][:, x % NCH, :, :], raw[s][:, x % COPIES, :, :],
                                            s_hi[s][:, x % NCH, :, :].bitcast(FP32), ALU.subtract).then_inc(lo_ready[s], 1)

            if normed:
                lines = "r (c n) -> (r c) n"
                sums_dram, inverse_dram = (x.rearrange(lines, c=P // (B * H)) for x in sources[0][1])
                pool.dma_start(packed[:, :], sums_dram).then_inc(packed_loaded, 16)
                pool.wait_ge(packed_ready, 1)
                pool.dma_start(inverse_dram, packed[:, :]).then_inc(packed_stored, 16)
                pool.wait_ge(packed_stored, 16)
            for x in range(COPIES):
                load(0, x)
            if rotary:
                gather(0, 0)
                pool.memset(ident[:, :], 0.0).then_inc(ident_ready, 1)
                pool.wait_ge(ident_ready, 1)
                pool.affine_select(out=ident[:, :], in_=ident[:, :], compare_op=ALU.not_equal, fill=1.0, base=0,
                                   pattern=[[-1, P]], channel_multiplier=1).then_inc(ident_ready, 1)
            low_parts(0, 0)
            with pool.Fori(0, B) as b:
                for hf in range(NCH):
                    n = b * NCH + hf
                    if residual is not None:
                        last = hf * NTILE + NTILE - 1
                        pool.wait_ge(bank_out[last % NB], b * ROUNDS)
                        pool.nop(nofuse=True)
                        pool.dma_start(res[:, hf, :, :], residual[bass.ds(b * D, D), hf * CH:(hf + 1) * CH].rearrange(
                            "(k p) n -> p k n", p=P)).then_inc(res_loaded[hf], 16)
                    load(b, hf + COPIES)
                    low_parts(b, hf + 1)
                    if rotary:
                        gather(b, hf + 1)
            for at in range(COPIES):
                for s in range(NS):
                    pool.wait_ge(raw_loaded[s][at], 16 * (B * NCH // COPIES + 1))
                if normed:
                    pool.wait_ge(inverse_loaded[at], P // DH * 16 * (B * NCH // COPIES + 1))
            if rotary:
                pool.wait_ge(rows_loaded, TB * 16 * (B * NCH + 1))

        @block.scalar
        def _(act):
            def high_parts(b, x):
                if x:
                    act.wait_ge(tile_ready, b * BODY + (x - 1) * NTILE)
                for s in range(NS):
                    if normed:
                        act.wait_ge(normed_ready, b * NCH + x + 1)
                    else:
                        act.wait_ge(raw_loaded[s][x % COPIES], loads(b, x) * 16)
                    nc.scalar.activation(s_hi[s][:, x % NCH, :, :], raw[s][:, x % COPIES, :, :], ACT.Copy
                                         ).then_inc(hi_ready[s], 1)

            high_parts(0, 0)
            if bias:
                act.wait_ge(bias_loaded, 16 * len(bias))
            with act.Fori(0, B) as b:
                for hf in range(NCH):
                    high_parts(b, hf + 1)
                    for g, k, t in tiles(hf):
                        if kind(g) not in "tr":
                            continue
                        slot = g % STAGES
                        act.wait_ge(tile_ready, b * BODY + g + 1)
                        act.wait_ge(stored[slot], b * stores(slot, BODY) + stores(slot, g))
                        if k in bias:
                            nc.scalar.activation(full[:, slot, :], bank[:, g % NB, :], ACT.Identity, bias=bias[k][:, t:t + 1]
                                                 ).then_inc(bank_out[g % NB], 1)
                        else:
                            nc.scalar.activation(full[:, slot, :], bank[:, g % NB, :], ACT.Copy
                                                 ).then_inc(bank_out[g % NB], 1)
                        if rotary and g % NTILE == 1:
                            n = b * NCH + hf
                            act.wait_ge(rows_turned, n + 1)
                            act.wait_ge(rope_done, (n + 2 - COPIES) * ROPE_CHUNK)
                            nc.scalar.activation(trig[:, hf % COPIES, :, :], trig_bank[:, :, :], ACT.Copy).then_inc(trig_ready, 1)

        @block.vector
        def _(dve):
            def normalise(b, x):
                at = x % COPIES
                dve.wait_ge(inverse_loaded[at], loads(b, x) * (P // DH * 16))
                dve.wait_ge(raw_loaded[0][at], loads(b, x) * 16)
                nc.vector.tensor_tensor(raw[0][:, at, :, :], raw[0][:, at, :, :], inverse[:, at, :, :], ALU.mult
                                        ).then_inc(normed_ready, 1)

            def rotate(b, g):
                hf = g // NTILE
                q = b * pairs_before(BODY) + pairs_before(g)
                dve.wait_ge(trig_ready, b * NCH + hf + 1)
                for half in (g, g + 1):
                    dve.wait_ge(bank_out[half % NB], out_of_bank(b, half))
                dve.wait_ge(tile_split, b * splits_before(BODY) + splits_before(g))
                first, second = full[:, g % STAGES, :], full[:, (g + 1) % STAGES, :]
                cos, sin = trig[:, hf % COPIES, 0, :], trig[:, hf % COPIES, 1, :]
                for r, (o, x, y, op) in enumerate((
                    (turn[:, 0, :], first, cos, ALU.mult),
                    (turn[:, 1, :], second, sin, ALU.mult),
                    (turn[:, 0, :], turn[:, 0, :], turn[:, 1, :], ALU.subtract),
                    (turn[:, 1, :], first, sin, ALU.mult),
                    (second, second, cos, ALU.mult),
                    (second, second, turn[:, 1, :], ALU.add),
                )):
                    if r in (2, 3, 5):
                        dve.wait_ge(rope_done, ROPE_CHUNK + q * ROPE_OPS + r)
                    nc.vector.tensor_tensor(o, x, y, op).then_inc(rope_done, 1)

            if normed:
                dve.wait_ge(packed_loaded, 16)
                nc.vector.reciprocal(packed[:, :], packed[:, :]).then_inc(packed_ready, 1)
                normalise(0, 0)
            for x in range(NW * KT):
                place, tile = x % WPLACES, (x // KT, x % KT)
                dve.wait_ge(w_loaded[place], 16 * (x // WPLACES + 1))
                nc.vector.tensor_copy(w_hi[tile[0]][:, tile[1], :], w_raw[:, place, :]).then_inc(w_hi_ready, 1)
                dve.wait_ge(w_hi_ready, x + 1)
                nc.vector.tensor_tensor(w_lo[tile[0]][:, tile[1], :], w_raw[:, place, :],
                                        w_hi[tile[0]][:, tile[1], :].bitcast(FP32), ALU.subtract).then_inc(w_ready, 1)
            if bias:
                dve.wait_ge(bias_loaded, 16 * len(bias))
            with dve.Fori(0, B) as b:
                for hf in range(NCH):
                    if normed:
                        normalise(b, hf + 1)
                    for g, k, t in tiles(hf):
                        what, slot = jobs[k][0], g % STAGES
                        if what in "tr":
                            e = b * splits_before(BODY) + splits_before(g)
                            if what == "t":
                                dve.wait_ge(bank_out[g % NB], out_of_bank(b, g))
                                src = full[:, slot, :]
                            else:
                                if t % 2 == 0:
                                    rotate(b, g)
                                q = b * pairs_before(BODY) + pairs_before(g - t % 2)
                                dve.wait_ge(rope_done, ROPE_CHUNK + (q + 1) * ROPE_OPS)
                                src = turn[:, 0, :] if t % 2 == 0 else full[:, slot, :]
                            dve.wait_ge(stored[slot], b * stores(slot, BODY) + stores(slot, g))
                            nc.vector.tensor_copy(hi[:, slot, :], src).then_inc(tile_hi, 1)
                            dve.wait_ge(tile_hi, e + 1)
                            nc.vector.tensor_tensor(lo[:, slot, :], src, hi[:, slot, :].bitcast(FP32), ALU.subtract
                                                    ).then_inc(tile_split, 1)
                            continue
                        dve.wait_ge(tile_ready, b * BODY + g + 1)
                        dve.wait_ge(stored[slot], b * stores(slot, BODY) + stores(slot, g))
                        if what == "v":
                            nc.vector.tensor_tensor(full[:, slot, :], bank[:, g % NB, :], bias[k][:, :], ALU.add
                                                    ).then_inc(bank_out[g % NB], 1)
                        else:
                            dve.wait_ge(res_loaded[hf], b * 16 + 16)
                            nc.vector.scalar_tensor_tensor(full[:, slot, :], bank[:, g % NB, :], bias[k][:, t:t + 1],
                                                           res[:, hf, t, :], ALU.add, ALU.add
                                                           ).then_inc(bank_out[g % NB], 1)

        @block.tensor
        def _(pe):
            if rotary:
                pe.sem_inc(rope_done, ROPE_CHUNK)
                pe.wait_ge(ident_ready, 2)
            with pe.Fori(0, B) as b:
                for hf in range(NCH):
                    seen = set()
                    for g, k, t in tiles(hf):
                        what, s = jobs[k][:2]
                        if t == 0:
                            pe.wait_ge(w_ready, (k + 1) * KT)
                        if s not in seen:
                            pe.wait_ge(lo_ready[s], b * NCH + hf + 1)
                            seen.add(s)
                        pe.wait_ge(bank_out[g % NB], b * ROUNDS + g // NB)
                        n = 0
                        for kt in range(KT):
                            for x, w in ((s_hi, w_hi), (s_hi, w_lo), (s_lo, w_hi)):
                                if what == "v":
                                    left, right = x[s][:, hf, kt, t * P:(t + 1) * P], w[k][:, kt, :]
                                else:
                                    left, right = w[k][:, kt, t * P:(t + 1) * P], x[s][:, hf, kt, :]
                                last = nc.tensor.matmul(bank[:, g % NB, :], left, right, start=(n == 0),
                                                        stop=(n == 3 * KT - 1))
                                n += 1
                        last.then_inc(tile_ready, 1)
                        if rotary and g % NTILE == 1:
                            n = b * NCH + hf
                            pe.wait_ge(rows_loaded, (n + 1) * (TB * 16))
                            pe.wait_ge(trig_ready, n)
                            for c in range(2):
                                for x in range(TB):
                                    last = nc.tensor.transpose(trig_bank[:, c, x * P:(x + 1) * P], rows[:, x, c, :], ident[:, :])
                            last.then_inc(rows_turned, 1)


RING = 4
SBANKS, TBANKS = 2, 2
PROBS = 8


def attend(nc, tag, q, k, v, att, sums, mask=None, scan=None):
    causal = mask is None
    SPB = RING if causal else 2 * PAIRS
    TURNS = NSTEP // SPB
    ROWS = 3 * DH
    SCAN = 4

    order = [t for pair in zip(range(KB - 1, -1, -1), range(KB // 2)) for t in pair]
    s_units = [(h, t, (t + 1) * P if causal else S) for h in range(2) for t in order]
    t_pairs = [(hf, j, q0, (hf + 1) * CH - q0) for hf in range(NCH) for j in range(KB)
               for q0 in [max(hf * CH, j * P) if causal else hf * CH] if q0 < (hf + 1) * CH]
    NS, NP = len(s_units), len(t_pairs)
    NT = 2 * NP
    assert NS == 2 * KB and KB % SBANKS == 0 and NT % PROBS == 0 and NP % 2 == 0
    last_of_half = [max(p for p, x in enumerate(t_pairs) if x[0] == hf) for hf in range(NCH)]
    first_of_half = [min(p for p, x in enumerate(t_pairs) if x[0] == hf) for hf in range(NCH)]
    EXPS0 = TBANKS
    USED0 = NP
    LOADS = 2 * ROWS // DH * 16

    with ExitStack() as ctx:
        m = Places(nc, ctx, tag)
        qs = m.sb("qs", [P, RING, 2, S], F32R)
        ks = m.sb("ks", [P, RING, 2, S], F32R)
        vs = m.sb("vs", [P, 2, KB, 2, 2 * DH])
        probs = m.sb("probs", [P, PROBS, CH])
        att_sb = m.sb("att_sb", [P, 2, NCH, CH])
        row_max = m.sb("row_max", [P, 2, 2 * KB])
        neg_max = m.sb("neg_max", [2 * KB, P], F32R)
        ident = m.sb("ident", [P, P])
        identb = m.sb("identb", [P, P], BF16)
        if causal:
            above = m.sb("above", [P, P], BF16)
            piece = m.sb("piece", [P, SCAN, S], U8)
            piece_f = m.sb("piece_f", [P, SCAN, S])
            masked = m.sb("masked", [P, SCAN, S])
            most_masked = m.sb("most_masked", [P, 1])
        else:
            bits = m.sb("bits", [P, KB, S], U8)
            addend = m.sb("addend", [P, 2, KB, S], BF16)
            found = m.sb("found", [1, P])
            most = m.sb("most", [1, 1])
            flag = m.sb("flag", [1, 1], I32)
        s_bank = m.ps("s_bank", [P, SBANKS, S])
        t_bank = m.ps("t_bank", [P, TBANKS, CH])
        acc = m.ps("acc", [P, NCH, CH])
        consts = m.sem("consts")
        row_ready = m.sem("row_ready")
        ones_ready = m.sem("ones_ready")
        qk_loaded = m.sems("qk_loaded", RING)
        v_loaded = m.sems("v_loaded", 2)
        mask_loaded = m.sem("mask_loaded")
        mask_ready = m.sem("mask_ready")
        found_loaded = m.sem("found_loaded")
        flag_ready = m.sem("flag_ready")
        scan_loaded = m.sem("scan_loaded")
        converted = m.sem("converted")
        scanned = m.sem("scanned")
        most_ready = m.sem("most_ready")
        scan_stored = m.sem("scan_stored")
        s_ready = m.sem("s_ready")
        s_free = m.sems("s_free", SBANKS)
        max_turned = m.sem("max_turned")
        neg_ready = m.sem("neg_ready")
        neg_loaded = m.sem("neg_loaded")
        t_ready = m.sem("t_ready")
        exps = m.sem("exps")
        used = m.sem("used")
        att_out = m.sems("att_out", NCH)
        att_stored = m.sems("att_stored", 2)
        block = m.block()

        def ring_uses(i, r):
            return i * (SPB // RING) + r // RING

        def maxima_schedule(r):
            return [(r + 1, s) for s in range(KB, NS)] + [(r + 2, 0), (r + 1, "turn")] + [(r + 2, s) for s in range(1, KB)]

        FIRST = [(0, s) for s in range(NS)] + [(1, 0), (0, "turn")] + [(1, s) for s in range(1, KB)]

        @block.sync
        def _(sp):
            def load_qk(i, r):
                n = (i * SPB + r) % NSTEP
                rows = bass.ds(n * 2 * DH, 2 * DH)
                for to, parts in ((qs, (0, 1, 0)), (ks, (0, 0, 1))):
                    src = q if to is qs else k
                    for j, part in enumerate(parts):
                        sp.dma_start(to[j * DH:(j + 1) * DH, r % RING, :, :].bitcast(FP32),
                                     src[part][rows, :].rearrange("(h d) n -> d h n", h=2)
                                     ).then_inc(qk_loaded[r % RING], 16)

            def load_v(i, r):
                n = (i * SPB + r) % NSTEP
                for h in range(2):
                    sp.dma_start(vs[:, r % 2, :, h, 0:DH],
                                 v[bass.ds(n, 1), :, h * DH:(h + 1) * DH].rearrange("a (j p) d -> p (a j) d", p=P)
                                 ).then_inc(v_loaded[r % 2], 16)

            def put_maxima(i, r):
                sp.wait_ge(neg_ready, i * SPB + r + 1)
                sp.dma_start(qs[ROWS:ROWS + 1, r % RING, :, :].bitcast(FP32).rearrange("a h (t n) -> a (h t) n", n=P),
                             neg_max[:, :].bitcast(FP32)).then_inc(neg_loaded, 16)

            def load_mask(b):
                sp.dma_start(bits[:, :, :], mask[0][bass.ds(b * KB, KB), :, :].rearrange("t p n -> p t n")
                             ).then_inc(mask_loaded, 16)

            load_qk(0, 0)
            load_qk(0, 1)
            load_v(0, 0)
            if not causal:
                sp.dma_start(found[:, :], mask[1].rearrange("p a -> a p")).then_inc(found_loaded, 16)
                load_mask(0)
            load_qk(0, 2)
            put_maxima(0, 0)
            with sp.Fori(0, TURNS) as i:
                for r in range(SPB):
                    n = i * SPB + r
                    sp.wait_ge(used, USED0 + n * NP)
                    load_qk(i, r + 3)
                    load_v(i, r + 1)
                    if not causal and r % PAIRS == 0:
                        b = i * (SPB // PAIRS) + r // PAIRS
                        sp.wait_ge(mask_ready, b + 1)
                        load_mask((b + 1) % B)
                    put_maxima(i, r + 1)
                    for hf in range(NCH):
                        sp.wait_ge(att_out[hf], n + 1 + hf)
                    for h in range(2):
                        at = 2 * h * DH
                        sp.dma_start(att[bass.ds((n * 2 + h) * DH, DH), :].rearrange("d (c n) -> d c n", c=NCH),
                                     att_sb[at:at + DH, r % 2, :, :]).then_inc(att_stored[r % 2], 16)
                        sp.dma_start(sums[bass.ds(n * 2 + h, 1), :].rearrange("d (c n) -> d c n", c=NCH),
                                     att_sb[at + DH:at + DH + 1, r % 2, :, :]).then_inc(att_stored[r % 2], 16)
            for r in range(RING):
                sp.wait_ge(qk_loaded[r], LOADS * (NSTEP // RING + (r < 3)))
            sp.wait_ge(v_loaded[0], 32 * (NSTEP // 2 + 1))
            sp.wait_ge(neg_loaded, 16 * (NSTEP + 1))
            if scan is not None:
                sp.wait_ge(most_ready, 1)
                sp.dma_start(scan[1], most_masked[:, :]).then_inc(scan_stored, 16)
                sp.wait_ge(scan_stored, 16)
            for x in range(2):
                sp.wait_ge(att_stored[x], 64 * (NSTEP // 2))

        @block.gpsimd
        def _(pool):
            pool.memset(ident[:, :], 0.0).then_inc(consts, 1)
            pool.memset(identb[:, :], 0.0).then_inc(consts, 1)
            pool.wait_ge(consts, 2)
            for x in (ident, identb):
                pool.affine_select(out=x[:, :], in_=x[:, :], compare_op=ALU.not_equal, fill=1.0, base=0,
                                   pattern=[[-1, P]], channel_multiplier=1).then_inc(consts, 1)
            if causal:
                pool.memset(above[:, :], 0.0).then_inc(consts, 1)
                pool.wait_ge(consts, 5)
                pool.affine_select(out=above[:, :], in_=above[:, :], compare_op=ALU.is_ge, fill=-BIG, base=0,
                                   pattern=[[-1, P]], channel_multiplier=1).then_inc(consts, 1)
            pool.wait_ge(consts, 6 if causal else 4)
            pool.memset(ks[ROWS:ROWS + 1, :, :, :].bitcast(FP32), 1.0).then_inc(row_ready, 1)
            pool.wait_ge(row_ready, 1)
            if scan is not None:
                pool.memset(masked[:, :, :], 0.0).then_inc(scanned, 1)
                with pool.Fori(0, B * KB // SCAN) as t:
                    pool.wait_ge(scanned, t + 1)
                    pool.nop(nofuse=True)
                    pool.dma_start(piece[:, :, :], scan[0][bass.ds(t * SCAN, SCAN), :, :].rearrange("t p n -> p t n")
                                   ).then_inc(scan_loaded, 16)
                    pool.wait_ge(scan_loaded, t * 16 + 16)
                    pool.nop(nofuse=True)
                    nc.gpsimd.tensor_copy(piece_f[:, :, :], piece[:, :, :]).then_inc(converted, 1)
                    pool.wait_ge(converted, t + 1)
                    nc.gpsimd.tensor_tensor(masked[:, :, :], masked[:, :, :], piece_f[:, :, :], ALU.add).then_inc(scanned, 1)
            if not causal:
                def addends(b, place):
                    pool.wait_ge(mask_loaded, b * 16 + 16)
                    pool.nop(nofuse=True)
                    nc.gpsimd.tensor_scalar(addend[:, place, :, :], bits[:, :, :], -BIG, None, ALU.mult
                                            ).then_inc(mask_ready, 1)

                addends(0, 0)
                with pool.Fori(0, TURNS) as i:
                    for place in range(SPB // PAIRS):
                        b = i * (SPB // PAIRS) + place
                        pool.wait_ge(used, USED0 + b * PAIRS * NP)
                        pool.nop(nofuse=True)
                        addends(b + 1, (place + 1) % 2)

        @block.scalar
        def _(act):
            def copy_out(place, hf):
                nc.scalar.activation(att_sb[:, place, hf, :], acc[:, hf, :], ACT.Copy).then_inc(att_out[hf], 1)

            act.wait_ge(ones_ready, 2)
            with act.Fori(0, TURNS) as i:
                for r in range(SPB):
                    n = i * SPB + r
                    for u in range(NT):
                        if u == 4:
                            act.wait_ge(used, USED0 + n * NP)
                            copy_out((r - 1) % 2, 1)
                        if u == 2 * last_of_half[0] + 6:
                            act.wait_ge(used, USED0 + n * NP + last_of_half[0] + 1)
                            act.wait_ge(att_stored[r % 2], (i * (SPB // 2) + r // 2) * 64)
                            copy_out(r % 2, 0)
                        w = t_pairs[u // 2][3]
                        act.wait_ge(t_ready, n * NT + u + 1)
                        act.wait_ge(used, USED0 + n * NP + (u - PROBS) // 2 + 1)
                        nc.scalar.activation(probs[:, u % PROBS, 0:w], t_bank[:, u % TBANKS, 0:w], ACT.Exp, scale=SCALE
                                             ).then_inc(exps, 1)
            act.wait_ge(used, USED0 + NSTEP * NP)
            copy_out(1, 1)

        @block.vector
        def _(dve):
            dve.memset(vs[:, :, :, :, DH:2 * DH], 1.0).then_inc(ones_ready, 1)
            dve.memset(acc[:, 1, :], 0.0).then_inc(ones_ready, 1)

            def maxima(i, r, s):
                n = i * SPB + r
                if s == "turn":
                    dve.wait_ge(max_turned, n + 1)
                    dve.wait_ge(neg_loaded, n * 16)
                    nc.vector.tensor_scalar(neg_max[:, :], s_bank[0:2 * KB, 1, 0:P], FLOOR, -1.0, ALU.max, ALU.mult
                                            ).then_inc(neg_ready, 1)
                    return
                h, t, w = s_units[s]
                dve.wait_ge(s_ready, n * NS + s + 1)
                nc.vector.tensor_reduce(row_max[:, r % 2, h * KB + t:h * KB + t + 1], s_bank[:, s % SBANKS, 0:w],
                                        AX.X, ALU.max).then_inc(s_free[s % SBANKS], 1)

            if not causal:
                dve.wait_ge(found_loaded, 16)
                nc.vector.tensor_reduce(most[:, :], found[:, :], AX.X, ALU.max).then_inc(flag_ready, 1)
                dve.wait_ge(flag_ready, 1)
                nc.vector.tensor_copy(flag[:, :], most[:, :]).then_inc(flag_ready, 1)
            for r, s in FIRST:
                maxima(0, r, s)
            with dve.Fori(0, TURNS) as i:
                for r in range(SPB):
                    for x, s in maxima_schedule(r):
                        maxima(i, x, s)
            if scan is not None:
                dve.wait_ge(scanned, B * KB // SCAN + 1)
                nc.vector.tensor_reduce(most_masked[:, :], masked[:, :, :], AX.XY, ALU.max).then_inc(most_ready, 1)

        @block.tensor
        def _(pe):
            pe.wait_ge(consts, 6 if causal else 4)
            pe.wait_ge(ones_ready, 2)
            pe.sem_inc(exps, EXPS0)
            pe.sem_inc(used, USED0)

            def add_mask(to, left, right):
                return nc.tensor.matmul(to, left, right, start=False, stop=True, skip_group_check=True)

            def by_query(i, r, s, masked):
                n = i * SPB + r
                if s == "turn":
                    for x in range(SBANKS):
                        pe.wait_ge(s_free[x], (n + 1) * (NS // SBANKS))
                    nc.tensor.transpose(s_bank[0:2 * KB, 1, 0:P], row_max[:, r % 2, :], ident[:, :]).then_inc(max_turned, 1)
                    return
                h, t, w = s_units[s]
                if s == 0:
                    pe.wait_ge(qk_loaded[r % RING], (ring_uses(i, r) + 1) * LOADS)
                    if masked and r % PAIRS == 0:
                        pe.wait_ge(mask_ready, i * (SPB // PAIRS) + r // PAIRS + 1)
                pe.wait_ge(s_free[s % SBANKS], n * (NS // SBANKS) + s // SBANKS)
                if s == 1:
                    pe.wait_ge(neg_ready, n)
                to = s_bank[:, s % SBANKS, :]
                for k0 in range(0, w, CH):
                    k1 = min(k0 + CH, w)
                    last = nc.tensor.matmul(to[:, k0:k1], qs[0:ROWS, r % RING, h, t * P:(t + 1) * P],
                                            ks[0:ROWS, r % RING, h, k0:k1], start=True, stop=True)
                    if masked:
                        last = add_mask(to[:, k0:k1], identb[:, :], addend[:, r // PAIRS % 2, t, k0:k1])
                if causal:
                    last = add_mask(to[:, t * P:(t + 1) * P], identb[:, :], above[:, :])
                last.then_inc(s_ready, 1)

            def by_key(i, r, p, masked):
                n, (hf, j, q0, w) = i * SPB + r, t_pairs[p]
                if p == 0:
                    pe.wait_ge(neg_loaded, n * 16 + 16)
                for h in range(2):
                    u = 2 * p + h
                    pe.wait_ge(exps, EXPS0 + n * NT + u - TBANKS + 1)
                    to = t_bank[:, u % TBANKS, :]
                    last = nc.tensor.matmul(to[:, 0:w], ks[0:ROWS + 1, r % RING, h, j * P:(j + 1) * P],
                                            qs[0:ROWS + 1, r % RING, h, q0:q0 + w], start=True, stop=True)
                    if causal and j * P >= hf * CH:
                        last = add_mask(to[:, 0:P], above[:, :], identb[:, :])
                    for x in range(w // P if masked else 0):
                        last = add_mask(to[:, x * P:(x + 1) * P], addend[:, r // PAIRS % 2, q0 // P + x, j * P:(j + 1) * P],
                                        identb[:, :])
                    last.then_inc(t_ready, 1)

            def values(i, r, p):
                n, (hf, j, q0, w) = i * SPB + r, t_pairs[p]
                if p == 0:
                    pe.wait_ge(v_loaded[r % 2], (i * (SPB // 2) + r // 2 + 1) * 32)
                if p == first_of_half[hf]:
                    pe.wait_ge(att_out[hf], n + hf)
                pe.wait_ge(exps, EXPS0 + n * NT + 2 * p + 2)
                at = q0 - hf * CH
                for h in range(2):
                    last = nc.tensor.matmul(acc[2 * DH * h:2 * DH * (h + 1), hf, at:at + w], vs[:, r % 2, j, h, :],
                                            probs[:, (2 * p + h) % PROBS, 0:w], start=j == 0, stop=True,
                                            skip_group_check=True)
                last.then_inc(used, 1)

            def steps(masked):
                for r, s in FIRST:
                    by_query(0, r, s, masked)
                pe.wait_ge(row_ready, 1)
                by_key(0, 0, 0, masked)
                with pe.Fori(0, TURNS) as i:
                    for r in range(SPB):
                        todo, asked = maxima_schedule(r), 0
                        for p in range(NP):
                            while asked * NP < (p + 1) * (NS + 1) and asked < NS + 1:
                                x, s = todo[asked]
                                by_query(i, x, s, masked)
                                asked += 1
                            by_key(i, r + (p + 1) // NP, (p + 1) % NP, masked)
                            values(i, r, p)

            if causal:
                steps(False)
            else:
                pe.wait_ge(flag_ready, 2)
                any_masked = pe.value_load(flag[0:1, 0:1])
                with pe.If(any_masked > 0):
                    steps(True)
                with pe.Else():
                    steps(False)


def feed_forward(nc, tag, att, sums, inverse, x, w, out):
    FT = FF // P
    PIECES = 2
    PT = CH // PIECES
    WF = 2
    WP = FT // WF
    NCHUNK = B * NCH
    START = [0, 8]
    SUMMED, HIGH, MEAN, CENTRED, SQUARED, VAR, ROOT, SCALED, DONE = 0, 0, 2, 2, 3, 4, 4, 5, 6

    def following(b, hf):
        return (b, hf + 1) if hf + 1 < NCH else ((b + 1) % B, 0)

    with ExitStack() as ctx:
        m = Places(nc, ctx, tag)
        w1_hi, w1_lo = (m.sb(f"w1_{x}", [P, KT, FF], F32R) for x in ("hi", "lo"))
        w2_hi, w2_lo = (m.sb(f"w2_{x}", [P, FT, D], F32R) for x in ("hi", "lo"))
        w_raw = m.sb("w_raw", [P, KT, CH])
        y_hi, y_lo = (m.sb(f"y_{x}", [P, NCH, KT, CH], F32R) for x in ("hi", "lo"))
        h = m.sb("h", [P, KT, PT])
        aux = m.sb("aux", [P, KT, PT])
        xin = m.sb("xin", [P, KT, PT])
        p_hi, p_lo = (m.sb(f"p_{x}", [P, KT, PT], F32R) for x in ("hi", "lo"))
        dev = m.sb("dev", [P, PT])
        gelu = m.sb("gelu", [P, 2, CH])
        packed = gelu[:, 0, :]
        assert CH == B * H * S // P
        g_hi, g_lo = (m.sb(f"g_{x}", [P, 2, CH], F32R) for x in ("hi", "lo"))
        assert KT * CH == 2 * WF * D
        mean_w = m.sb("mean_w", [P, P], F32R)
        mean_f = m.sb("mean_f", [P, P])
        eps = m.sb("eps", [P, 1])
        b1 = m.sb("b1", [P, FT])
        b2, gain, shift = (m.sb(x, [P, KT]) for x in ("b2", "gain", "shift"))
        acc = m.ps("acc", [P, KT, CH])
        hid = m.ps("hid", [P, 2, CH])
        stat = m.ps("stat", [P, 2, CH])
        w_loaded = m.sems("w_loaded", 2)
        w_hi_ready = m.sem("w_hi_ready")
        w_ready = m.sem("w_ready")
        vec_loaded = m.sem("vec_loaded")
        consts = m.sem("consts")
        packed_loaded = m.sem("packed_loaded")
        packed_ready = m.sem("packed_ready")
        packed_stored = m.sem("packed_stored")
        x_loaded = m.sem("x_loaded")
        inverse_loaded = m.sem("inverse_loaded")
        att_loaded = m.sem("att_loaded")
        ln_dve = m.sem("ln_dve")
        ln_hi = m.sem("ln_hi")
        ln_lo = m.sem("ln_lo")
        ln_stat = m.sem("ln_stat")
        squared = m.sem("squared")
        rooted = m.sem("rooted")
        y_hi_ready = m.sem("y_hi_ready")
        y_ready = m.sem("y_ready")
        hid_ready = m.sem("hid_ready")
        gelu_ready = m.sems("gelu_ready", 2)
        g_hi_ready = m.sem("g_hi_ready")
        g_ready = m.sems("g_ready", 2)
        g_used = m.sems("g_used", 2)
        acc_out = m.sem("acc_out")
        x_ready = m.sem("x_ready")
        stored = m.sems("stored", KT)
        block = m.block()
        DVE_STEPS = 2 + 1 + 2 + KT

        def raw_piece(k):
            half = w_raw[:, k % 2 * KT // 2:(k % 2 + 1) * KT // 2, :].rearrange("p a n -> p (a n)")
            return half.rearrange("p (k n) -> p k n", k=KT if k % 2 == 0 else WF)

        def at(slot, step):
            return [p for p in range(PIECES) if START[p] + step == slot]

        @block.sync
        def _(sp):
            def load_x(b, c):
                sp.dma_start(xin[:, :, :], x[bass.ds(b * D, D), c].rearrange("(k p) n -> p k n", p=P)).then_inc(x_loaded, 16)

            def load_inverse(b, c):
                for to, src in by_head(inverse, b, c, aux):
                    sp.dma_start(to, src).then_inc(inverse_loaded, 16)

            def load_att(b, c):
                sp.dma_start(h[:, :, :], att[bass.ds(b * D, D), c].rearrange("(k p) n -> p k n", p=P)
                             ).then_inc(att_loaded, 16)

            def load_after(q, b, hf, p):
                c = slice(hf * CH + p * PT, hf * CH + (p + 1) * PT)
                sp.wait_ge(ln_dve, q * DVE_STEPS + 2)
                load_x(b, c)
                sp.wait_ge(ln_lo, 2 * q + 2)
                load_inverse(b, c)
                sp.wait_ge(y_ready, q + 1)
                load_att(b, c)

            lines = "r (c n) -> (r c) n"
            sp.dma_start(packed, sums.rearrange(lines, c=P // (B * H))).then_inc(packed_loaded, 16)
            for to, src in ((b1, w["b1"]), (b2, w["b2"]), (gain, w["g"]), (shift, w["beta"])):
                sp.dma_start(to[:, :], src).then_inc(vec_loaded, 16)
            def load_weights(pieces):
                for k in pieces:
                    if k >= 2:
                        sp.wait_ge(w_ready, k - 1)
                    if k % 2 == 0:
                        src = w["W1"].rearrange("(k p) n -> p k n", p=P)[:, :, k // 2 * WF * P:(k // 2 + 1) * WF * P]
                    else:
                        src = w["W2"].rearrange("(k p) n -> p k n", p=P)[:, k // 2 * WF:(k // 2 + 1) * WF, :]
                    sp.dma_start(raw_piece(k), src).then_inc(w_loaded[k % 2], 16)

            load_x(0, slice(0, PT))
            load_att(0, slice(0, PT))
            load_weights(range(2))
            sp.wait_ge(packed_ready, 1)
            sp.dma_start(inverse.rearrange(lines, c=P // (B * H)), packed).then_inc(packed_stored, 16)
            sp.wait_ge(packed_stored, 16)
            load_inverse(0, slice(0, PT))
            load_weights(range(2, 5))
            load_after(0, 0, 0, 1)
            load_weights(range(5, 11))
            load_after(1, *following(0, 0), 0)
            load_weights(range(11, 2 * WP))
            with sp.Fori(0, B) as b:
                for hf in range(NCH):
                    n = b * NCH + hf
                    load_after(PIECES * (n + 1), *following(b, hf), 1)
                    load_after(PIECES * (n + 1) + 1, (b + 1) % B, hf, 0)
                    for t in range(KT):
                        sp.wait_ge(x_ready, n * KT + t + 1)
                        sp.nop(nofuse=True)
                        sp.dma_start(out[bass.ds(b * D + t * P, P), hf * CH:(hf + 1) * CH], w_raw[:, t, :]
                                     ).then_inc(stored[t], 16)
            for t in range(KT):
                sp.wait_ge(stored[t], 16 * NCHUNK)
            loads = PIECES * (NCHUNK + 1) + 1
            sp.wait_ge(x_loaded, 16 * loads)
            sp.wait_ge(inverse_loaded, P // DH * 16 * loads)
            sp.wait_ge(att_loaded, 16 * loads)

        @block.gpsimd
        def _(pool):
            def low_parts(hf, p, q):
                for k, src in ((0, h), (1, aux)):
                    pool.wait_ge(ln_hi, 2 * q + k + 1)
                    nc.gpsimd.tensor_tensor(p_lo[:, :, :], src[:, :, :], p_hi[:, :, :].bitcast(FP32), ALU.subtract
                                            ).then_inc(ln_lo, 1)
                pool.wait_ge(y_hi_ready, q + 1)
                nc.gpsimd.tensor_tensor(y_lo[:, hf, :, p * PT:(p + 1) * PT], h[:, :, :],
                                        y_hi[:, hf, :, p * PT:(p + 1) * PT].bitcast(FP32), ALU.subtract
                                        ).then_inc(y_ready, 1)

            for p in range(PIECES):
                low_parts(0, p, p)
            with pool.Fori(0, B) as b:
                for hf in range(NCH):
                    n = b * NCH + hf
                    for p in range(PIECES):
                        low_parts((hf + 1) % NCH, p, PIECES * (n + 1) + p)
                    for t in range(KT):
                        pool.wait_ge(acc_out, n * KT + t + 1)
                        nc.gpsimd.tensor_tensor(w_raw[:, t, :], w_raw[:, t, :], y_lo[:, hf, t, :].bitcast(FP32), ALU.add
                                                ).then_inc(x_ready, 1)

        @block.scalar
        def _(act):
            def high(hf, p, q):
                act.wait_ge(ln_dve, q * DVE_STEPS + 2)
                nc.scalar.activation(p_hi[:, :, :], h[:, :, :], ACT.Copy).then_inc(ln_hi, 1)

            def square(hf, p, q):
                act.wait_ge(ln_dve, q * DVE_STEPS + 3)
                nc.scalar.activation(aux[:, :, :], h[:, :, :], ACT.Square).then_inc(squared, 1)
                act.wait_ge(squared, q + 1)
                nc.scalar.activation(p_hi[:, :, :], aux[:, :, :], ACT.Copy).then_inc(ln_hi, 1)

            def root(hf, p, q):
                act.wait_ge(ln_stat, 2 * q + 2)
                nc.scalar.activation(dev[:, :], stat[:, 1, 0:PT], ACT.Sqrt, bias=eps[:, :]).then_inc(rooted, 1)

            def y_high(hf, p, q, chunks):
                act.wait_ge(ln_dve, (q + 1) * DVE_STEPS)
                if chunks is not None:
                    act.wait_ge(x_ready, chunks * KT)
                nc.scalar.activation(y_hi[:, hf, :, p * PT:(p + 1) * PT], h[:, :, :], ACT.Copy).then_inc(y_hi_ready, 1)

            act.wait_ge(vec_loaded, 64)
            act.wait_ge(consts, 3)
            for p in range(PIECES):
                high(0, p, p)
                square(0, p, p)
                root(0, p, p)
                y_high(0, p, p, None)
            with act.Fori(0, B) as b:
                for hf in range(NCH):
                    n = b * NCH + hf
                    nxt = (hf + 1) % NCH
                    for f in range(FT):
                        act.wait_ge(hid_ready, n * FT + f + 1)
                        act.wait_ge(g_ready[f % 2], n * (FT // 2) + f // 2)
                        nc.scalar.activation(gelu[:, f % 2, :], hid[:, f % 2, :], ACT.Gelu, bias=b1[:, f:f + 1]
                                             ).then_inc(gelu_ready[f % 2], 1)
                        q = PIECES * (n + 1)
                        for p in at(f, HIGH):
                            high(nxt, p, q + p)
                        for p in at(f, SQUARED):
                            square(nxt, p, q + p)
                        for p in at(f, ROOT):
                            root(nxt, p, q + p)
                        for p in at(f, DONE):
                            y_high(nxt, p, q + p, n)

        @block.vector
        def _(dve):
            def spread(v):
                return v.unsqueeze(1).to_broadcast([P, KT, PT])

            def summed(q):
                s = q * DVE_STEPS
                dve.wait_ge(att_loaded, (q + 1) * 16)
                dve.wait_ge(inverse_loaded, (q + 1) * (P // DH * 16))
                dve.wait_ge(x_loaded, (q + 1) * 16)
                nc.vector.tensor_tensor(h[:, :, :], h[:, :, :], aux[:, :, :], ALU.mult).then_inc(ln_dve, 1)
                dve.wait_ge(ln_dve, s + 1)
                nc.vector.tensor_tensor(h[:, :, :], h[:, :, :], xin[:, :, :], ALU.add).then_inc(ln_dve, 1)

            def centred(q):
                dve.wait_ge(ln_stat, 2 * q + 1)
                nc.vector.tensor_tensor(h[:, :, :], h[:, :, :], spread(stat[:, 0, 0:PT]), ALU.subtract).then_inc(ln_dve, 1)

            def scaled(q):
                s = q * DVE_STEPS + 3
                dve.wait_ge(rooted, q + 1)
                nc.vector.reciprocal(dev[:, :], dev[:, :]).then_inc(ln_dve, 1)
                dve.wait_ge(ln_dve, s + 1)
                nc.vector.tensor_tensor(h[:, :, :], h[:, :, :], spread(dev[:, :]), ALU.mult).then_inc(ln_dve, 1)
                dve.wait_ge(ln_dve, s + 2)
                for k in range(KT):
                    nc.vector.tensor_scalar(h[:, k, :], h[:, k, :], gain[:, k:k + 1], shift[:, k:k + 1], ALU.mult, ALU.add
                                            ).then_inc(ln_dve, 1)

            dve.wait_ge(packed_loaded, 16)
            nc.vector.reciprocal(packed, packed).then_inc(packed_ready, 1)
            dve.memset(mean_f[:, :], 1.0 / D).then_inc(consts, 1)
            dve.memset(eps[:, :], LN_EPS).then_inc(consts, 1)
            dve.wait_ge(consts, 2)
            nc.vector.tensor_copy(mean_w[:, :], mean_f[:, :]).then_inc(consts, 1)
            dve.wait_ge(vec_loaded, 64)

            def split_piece(k):
                to_hi, to_lo = ((w1_hi, w1_lo), (w2_hi, w2_lo))[k % 2]
                c = k // 2
                part = (slice(None), slice(None), slice(c * WF * P, (c + 1) * WF * P)) if k % 2 == 0 else (
                    slice(None), slice(c * WF, (c + 1) * WF), slice(None))
                dve.wait_ge(w_loaded[k % 2], 16 * (k // 2 + 1))
                nc.vector.tensor_copy(to_hi[part], raw_piece(k)).then_inc(w_hi_ready, 1)
                dve.wait_ge(w_hi_ready, k + 1)
                nc.vector.tensor_tensor(to_lo[part], raw_piece(k), to_hi[part].bitcast(FP32), ALU.subtract
                                        ).then_inc(w_ready, 1)

            def split_weights(pieces):
                for k in pieces:
                    split_piece(k)

            split_weights(range(0, 2))
            summed(0)
            split_weights(range(2, 3))
            centred(0)
            split_weights(range(3, 4))
            scaled(0)
            split_weights(range(4, 5))
            summed(1)
            split_weights(range(5, 7))
            centred(1)
            split_weights(range(7, 9))
            scaled(1)
            split_weights(range(9, 2 * WP))
            with dve.Fori(0, B) as b:
                for hf in range(NCH):
                    n = b * NCH + hf
                    q = PIECES * (n + 1)
                    for f in range(FT):
                        s = f % 2
                        dve.wait_ge(gelu_ready[s], n * (FT // 2) + f // 2 + 1)
                        dve.wait_ge(g_used[s], n * (FT // 2) + f // 2)
                        nc.vector.tensor_copy(g_hi[:, s, :], gelu[:, s, :]).then_inc(g_hi_ready, 1)
                        dve.wait_ge(g_hi_ready, n * FT + f + 1)
                        nc.vector.tensor_tensor(g_lo[:, s, :], gelu[:, s, :], g_hi[:, s, :].bitcast(FP32), ALU.subtract
                                                ).then_inc(g_ready[s], 1)
                        for p in at(f, SUMMED):
                            summed(q + p)
                        for p in at(f, CENTRED):
                            centred(q + p)
                        for p in at(f, SCALED):
                            scaled(q + p)
                    for t in range(KT):
                        dve.wait_ge(g_used[1], (n + 1) * (FT // 2))
                        dve.wait_ge(stored[t], n * 16)
                        nc.vector.scalar_tensor_tensor(w_raw[:, t, :], acc[:, t, :], b2[:, t:t + 1],
                                                       y_hi[:, hf, t, :].bitcast(FP32), ALU.add, ALU.add).then_inc(acc_out, 1)

        @block.tensor
        def _(pe):
            def statistic(k, q):
                pe.wait_ge(ln_lo, 2 * q + k + 1)
                n = 0
                for part in (p_hi, p_lo):
                    for t in range(KT):
                        last = nc.tensor.matmul(stat[:, k, 0:PT], mean_w[:, :], part[:, t, :], start=n == 0,
                                                stop=n == 2 * KT - 1)
                        n += 1
                last.then_inc(ln_stat, 1)

            def product(to, left, right, first, last_one):
                n, count = 0, 3 * len(left)
                for (l_hi, l_lo), (r_hi, r_lo) in zip(left, right):
                    for l, r in ((l_hi, r_hi), (l_lo, r_hi), (l_hi, r_lo)):
                        last = nc.tensor.matmul(to, l, r, start=first and n == 0, stop=last_one and n == count - 1)
                        n += 1
                return last

            def hidden(hf, n, f):
                pe.wait_ge(w_ready, 2 * (f // WF) + 1)
                if f == 0:
                    pe.wait_ge(y_ready, PIECES * (n + 1))
                pe.wait_ge(gelu_ready[f % 2], n * (FT // 2) + f // 2)
                c = slice(f * P, (f + 1) * P)
                product(hid[:, f % 2, :], [(w1_hi[:, k, c], w1_lo[:, k, c]) for k in range(KT)],
                        [(y_hi[:, hf, k, :], y_lo[:, hf, k, :]) for k in range(KT)], True, True).then_inc(hid_ready, 1)

            def output(n, f):
                pe.wait_ge(w_ready, 2 * (f // WF) + 2)
                pe.wait_ge(g_ready[f % 2], n * (FT // 2) + f // 2 + 1)
                for t in range(KT):
                    if f == 0:
                        pe.wait_ge(acc_out, n * KT)
                    c = slice(t * P, (t + 1) * P)
                    last = product(acc[:, t, :], [(w2_hi[:, f, c], w2_lo[:, f, c])], [(g_hi[:, f % 2, :], g_lo[:, f % 2, :])],
                                   f == 0, f == FT - 1)
                last.then_inc(g_used[f % 2], 1)

            pe.wait_ge(consts, 3)
            for p in range(PIECES):
                statistic(0, p)
                statistic(1, p)
            with pe.Fori(0, B) as b:
                for hf in range(NCH):
                    n = b * NCH + hf
                    hidden(hf, n, 0)
                    for f in range(FT):
                        for p in at(f, MEAN):
                            statistic(0, PIECES * (n + 1) + p)
                        for p in at(f, VAR):
                            statistic(1, PIECES * (n + 1) + p)
                        if f + 1 < FT:
                            hidden(hf, n, f + 1)
                        output(n, f)


def program(nc, a, out):
    def dram(name, shape, dtype=FP32):
        return nc.dram_tensor(f"scratch_{name}", shape, dtype, kind="Internal").ap()

    rope = (a["tokens"], a["trig"])
    any_masked = dram("any_masked", [P, 1])
    q0h, q0l, k0h, k0l, k1h, k1l, q1h, q1l = (dram(n, [B * D, S]) for n in
                                              ("q0h", "q0l", "k0h", "k0l", "k1h", "k1l", "q1h", "q1l"))
    v0, v1 = (dram(n, [NSTEP, S, 2 * DH]) for n in ("v0", "v1"))
    project(nc, "proj", [(a["x"], None), (a["ctx"], None)], [
        ("t", 0, a["Wq0"], a["bq0"], (q0h, q0l)),
        ("r", 1, a["Wk1"], None, (k1h, k1l)),
        ("t", 1, a["Wk0"], a["bk0"], (k0h, k0l)),
        ("v", 1, a["Wv0"], a["bv0"], (v0,)),
        ("v", 1, a["Wv1"], a["bv1"], (v1,)),
    ], rope)
    att0, att1 = (dram(n, [B * D, S]) for n in ("att0", "att1"))
    sum0, sum1, inv0, inv1 = (dram(n, [B * H, S]) for n in ("sum0", "sum1", "inv0", "inv1"))
    attend(nc, "att0", (q0h, q0l), (k0h, k0l), v0, att0, sum0, scan=(a["mask"], any_masked))
    x1 = dram("x1", [B * D, S])
    feed_forward(nc, "ffn", att0, sum0, inv0, a["x"], a, x1)
    project(nc, "q1", [(x1, None)], [("r", 0, a["Wq1"], a["bq1"], (q1h, q1l))], rope)
    attend(nc, "att1", (q1h, q1l), (k1h, k1l), v1, att1, sum1, (a["mask"], any_masked))
    project(nc, "out", [(att1, (sum1, inv1))], [("o", 0, a["Wo"], a["bo"], (out, x1))])


def kernel(**inputs):
    import concourse.bacc as bacc
    from concourse.bass_utils import run_bass_kernel_spmd

    f = {k: np.asarray(v) for k, v in inputs.items()}

    def turned(v):
        return np.ascontiguousarray(np.swapaxes(v, -1, -2))

    def columns(v):
        return np.ascontiguousarray(v.reshape(-1, P).T)

    def rows(v):
        return np.ascontiguousarray(np.broadcast_to(v, (P, v.size)))

    def halves(v):
        return np.ascontiguousarray(v.reshape(-1, H // 8, 8, 2, DH // 2).transpose(0, 1, 3, 2, 4).reshape(v.shape))

    inv_freq = np.float32(1.0) / np.power(np.float32(10000.0), np.arange(0, DH, 2, dtype=np.float32) / np.float32(DH))
    angle = np.arange(MAX_POS, dtype=np.float32)[:, None] * inv_freq[None]
    trig = np.concatenate([np.tile(np.cos(angle), (1, 8)), np.tile(np.sin(angle), (1, 8))], axis=1).astype(np.float32)

    arrays = {
        "x": turned(f["x"]).reshape(B * D, S),
        "ctx": turned(f["ctx_1024"]).reshape(B * D, S),
        "tokens": np.ascontiguousarray(f["itok_BxS2_0_2047"].reshape(B * KB, P).T).view(np.uint32),
        "trig": trig,
        "mask": np.ascontiguousarray(f["mask_BxSxS2_bf0"]).reshape(B * KB, P, S),
        "Wq0": turned(f["L0_xattn_Wq"]), "bq0": columns(f["L0_xattn_bq"]),
        "Wk0": turned(f["L0_xattn_Wk"]), "bk0": columns(f["L0_xattn_bk"]),
        "Wv0": turned(f["L0_xattn_Wv"]), "bv0": rows(f["L0_xattn_bv"]),
        "W1": turned(f["L0_xattn_W1"]), "b1": columns(f["L0_xattn_b1"]),
        "W2": turned(f["L0_xattn_W2"]), "b2": columns(f["L0_xattn_b2"]),
        "g": columns(f["L0_xattn_ln_g"]), "beta": columns(f["L0_xattn_ln_b"]),
        "Wq1": halves(f["L1_xattn_q_w"]), "bq1": columns(halves(f["L1_xattn_q_b"])),
        "Wk1": halves(f["L1_xattn_k_w"]),
        "Wv1": np.ascontiguousarray(f["L1_xattn_v_w"]), "bv1": rows(f["L1_xattn_v_b"]),
        "Wo": np.ascontiguousarray(f["L1_xattn_proj_w"]), "bo": columns(f["L1_xattn_proj_b"]),
    }
    nc = bacc.Bacc("TRN2", target_bir_lowering=False, num_devices=1)
    a = {k: nc.dram_tensor(f"in_{k}", v.shape, mybir.dt.from_np(v.dtype), kind="ExternalInput").ap()
         for k, v in arrays.items()}
    out = nc.dram_tensor("out", (B * D, S), FP32, kind="ExternalOutput").ap()
    program(nc, a, out)
    r = run_bass_kernel_spmd(nc, [{f"in_{k}": v for k, v in arrays.items()}], core_ids=[0])
    return turned(np.asarray(r.results[0]["out"]).reshape(B, D, S))
```
